# Optimizing a Trainium2 kernel written in Bass

```python
import numpy as np
import jax
import jax.numpy as jnp

def _softmax(x, axis=-1):
    return jax.nn.softmax(x, axis=axis)
def _gelu(x):
    return jax.nn.gelu(x, approximate=True)
def _silu(x):
    return jax.nn.silu(x)
def _sigmoid(x):
    return jax.nn.sigmoid(x)
def _layernorm(x, axis=-1, eps=1e-5):
    m = jnp.mean(x, axis=axis, keepdims=True)
    v = jnp.var(x, axis=axis, keepdims=True)
    return (x - m) / jnp.sqrt(v + eps)
def _scatter_add(tgt, idx, src, axis=0):
    return tgt.at[idx].add(src)
def _segment_sum(src, seg, n):
    return jax.ops.segment_sum(src, seg, n)

kernel_name = 'mk_conv_preact_d2_conv_nhwc32_59e938'

def setup_inputs(seed: int = 0):
    np.random.seed(seed)
    _w = jnp.asarray
    def _rec_inputs():
        import jax
        import jax.numpy as jnp
        _gk = jax.random.key(seed)
        x = -0.000125 + 0.9999 * jax.random.normal(jax.random.fold_in(_gk, 1), (16, 256, 256, 32), jnp.float32)
        return x
    x = _rec_inputs()
    def _L0_conv_setup():
        import jax, jax.numpy as jnp
        import numpy as np
        N_PIXELS = 256
        MODE_THRESHOLD = 16.0
        N_IN, N_OUT = (32, 32)
        BATCH = 16

        def _mode_idx():
            fx, fy = np.meshgrid(np.fft.rfftfreq(N_PIXELS, 1 / N_PIXELS), np.fft.fftfreq(N_PIXELS, 1 / N_PIXELS))
            mask = fx ** 2 + fy ** 2 <= MODE_THRESHOLD ** 2
            i0, i1 = np.where(mask)
            return (i0.astype(np.int32), i1.astype(np.int32))
        key = jax.random.key(seed)
        kx, kre, kim = jax.random.split(key, 3)
        i0, i1 = _mode_idx()
        m = i0.shape[0]
        s = 1.0 / (N_IN * N_OUT)
        return {'x': jax.random.normal(kx, (BATCH, N_PIXELS, N_PIXELS, N_IN), dtype=jnp.float32), 'w_re': jax.random.uniform(kre, (m, N_IN, N_OUT), minval=-s, maxval=s, dtype=jnp.float32), 'w_im': jax.random.uniform(kim, (m, N_IN, N_OUT), minval=-s, maxval=s, dtype=jnp.float32), 'idx0': jnp.asarray(i0), 'idx1': jnp.asarray(i1)}
    _L0_conv_all = _L0_conv_setup()
    _L0_conv_in = {k: v for k, v in _L0_conv_all.items() if k in ('w_re', 'w_im', 'idx0', 'idx1', )}
    del _L0_conv_all

    def _L1_conv_setup():
        import jax, jax.numpy as jnp
        import numpy as np
        from jax import lax
        MAX_SCALE = 4
        SCALES = [2 ** i for i in range(1, MAX_SCALE + 1)]
        EPS_K = 1e-07
        BN_EPS = 0.001

        def sample_min_max_scaling(x):
            mn = jnp.min(x, axis=(1, 2, 3), keepdims=True)
            mx = jnp.max(x, axis=(1, 2, 3), keepdims=True)
            return (x - mn) / (mx - mn + EPS_K)

        def box_sum(x, r):
            c = x.shape[-1]
            kernel = jnp.ones((r, r, 1, c), dtype=x.dtype)
            return lax.conv_general_dilated(x, kernel, window_strides=(1, 1), padding='SAME', dimension_numbers=('NHWC', 'HWIO', 'NHWC'), feature_group_count=c)
        key = jax.random.key(seed)
        B, H, W, C = (16, 224, 224, 32)
        x = jax.random.normal(key, (B, H, W, C), dtype=jnp.float32)
        return {'x': x, 'gamma': jnp.ones((C,), jnp.float32), 'beta': jnp.zeros((C,), jnp.float32), 'moving_mean': jnp.zeros((C,), jnp.float32), 'moving_var': jnp.ones((C,), jnp.float32)}
    _L1_conv_all = _L1_conv_setup()
    _L1_conv_in = {k: v for k, v in _L1_conv_all.items() if k in ('gamma', 'beta', 'moving_mean', 'moving_var', )}
    del _L1_conv_all

    return {
        "x": x,
        "L0_conv_w_re": _L0_conv_in["w_re"],
        "L0_conv_w_im": _L0_conv_in["w_im"],
        "L0_conv_idx0": _L0_conv_in["idx0"],
        "L0_conv_idx1": _L0_conv_in["idx1"],
        "L1_conv_gamma": _L1_conv_in["gamma"],
        "L1_conv_beta": _L1_conv_in["beta"],
        "L1_conv_moving_mean": _L1_conv_in["moving_mean"],
        "L1_conv_moving_var": _L1_conv_in["moving_var"],
    }

def reference(x, L0_conv_w_re, L0_conv_w_im, L0_conv_idx0, L0_conv_idx1, L1_conv_gamma, L1_conv_beta, L1_conv_moving_mean, L1_conv_moving_var):
    import jax
    import jax.numpy as jnp
    def _L0_conv_ref(x, w_re, w_im, idx0, idx1):
        import jax, jax.numpy as jnp
        import numpy as np
        N_PIXELS = 256
        MODE_THRESHOLD = 16.0
        N_IN, N_OUT = (32, 32)
        BATCH = 16

        def _mode_idx():
            fx, fy = np.meshgrid(np.fft.rfftfreq(N_PIXELS, 1 / N_PIXELS), np.fft.fftfreq(N_PIXELS, 1 / N_PIXELS))
            mask = fx ** 2 + fy ** 2 <= MODE_THRESHOLD ** 2
            i0, i1 = np.where(mask)
            return (i0.astype(np.int32), i1.astype(np.int32))
        x_fft = jnp.fft.rfft2(x, axes=(-3, -2))
        x_sel = x_fft[:, idx0, idx1, :]
        w = (w_re + 1j * w_im).astype(x_fft.dtype)
        y_sel = jnp.einsum('bfi,fio->bfo', x_sel, w)
        y_fft = jnp.zeros((x.shape[0], x_fft.shape[1], x_fft.shape[2], w.shape[-1]), dtype=x_fft.dtype)
        y_fft = y_fft.at[:, idx0, idx1, :].set(y_sel)
        return jnp.fft.irfft2(y_fft, axes=(-3, -2))

    def _L1_conv_ref(x, gamma, beta, moving_mean, moving_var):
        import jax, jax.numpy as jnp
        import numpy as np
        from jax import lax
        MAX_SCALE = 4
        SCALES = [2 ** i for i in range(1, MAX_SCALE + 1)]
        EPS_K = 1e-07
        BN_EPS = 0.001

        def sample_min_max_scaling(x):
            mn = jnp.min(x, axis=(1, 2, 3), keepdims=True)
            mx = jnp.max(x, axis=(1, 2, 3), keepdims=True)
            return (x - mn) / (mx - mn + EPS_K)

        def box_sum(x, r):
            c = x.shape[-1]
            kernel = jnp.ones((r, r, 1, c), dtype=x.dtype)
            return lax.conv_general_dilated(x, kernel, window_strides=(1, 1), padding='SAME', dimension_numbers=('NHWC', 'HWIO', 'NHWC'), feature_group_count=c)
        x = sample_min_max_scaling(x)
        measures = jnp.stack([box_sum(x, r) for r in SCALES], axis=-1)
        log_scales = jnp.log(jnp.asarray(SCALES, dtype=x.dtype))
        log_measures = jnp.log(measures + EPS_K)
        mean_ls = jnp.mean(log_scales)
        mean_lm = jnp.mean(log_measures, axis=-1, keepdims=True)
        dls = log_scales - mean_ls
        num = jnp.sum((log_measures - mean_lm) * dls, axis=-1)
        den = jnp.sum(dls ** 2)
        alphas = num / den
        return (alphas - moving_mean) / jnp.sqrt(moving_var + BN_EPS) * gamma + beta

    def _gn(v, G=16, eps=1e-5):
        B_, H_, W_, C_ = v.shape
        g = v.reshape(B_, H_, W_, G, C_ // G)
        m = jnp.mean(g, axis=(1, 2, 4), keepdims=True)
        s = jnp.var(g, axis=(1, 2, 4), keepdims=True)
        return ((g - m) / jnp.sqrt(s + eps)).reshape(v.shape)

    def _ln_c(v, eps=1e-6):
        m = jnp.mean(v, axis=-1, keepdims=True)
        s = jnp.var(v, axis=-1, keepdims=True)
        return (v - m) / jnp.sqrt(s + eps)

    def _ln_t(v, eps=1e-5):
        m = jnp.mean(v, axis=-1, keepdims=True)
        s = jnp.var(v, axis=-1, keepdims=True)
        return (v - m) / jnp.sqrt(s + eps)

    def _to_tokens(v):
        B_, H_, W_, C_ = v.shape
        return v.reshape(B_, H_ * W_, C_)
    def _from_tokens(t, like):
        return t.reshape(like.shape)

    x = x + _L0_conv_ref(_gn(x), L0_conv_w_re, L0_conv_w_im, L0_conv_idx0, L0_conv_idx1)
    x = x + _L1_conv_ref(_gn(x), L1_conv_gamma, L1_conv_beta, L1_conv_moving_mean, L1_conv_moving_var)
    return x


_drawn_inputs = setup_inputs


def setup_inputs(seed=0):
    import zlib

    import numpy as np

    out = dict(_drawn_inputs(seed))
    spreads = {'L1_conv_gamma': (1.0, 0.2),
     'L1_conv_beta': (0.0, 0.1),
     'L1_conv_moving_mean': (0.0, 0.1),
     'L1_conv_moving_var': (1.0, 0.2)}
    factors = {'L0_conv_w_re': 200.0, 'L0_conv_w_im': 200.0}
    for name, (base, spread) in spreads.items():
        noise = np.random.default_rng([zlib.crc32(name.encode()), seed]).standard_normal(out[name].shape)
        drawn = base * np.exp(spread * noise) if base else spread * noise
        out[name] = jnp.asarray(drawn.astype(out[name].dtype))
    for name, factor in factors.items():
        out[name] = (out[name] * factor).astype(out[name].dtype)
    return out
```

```python
from contextlib import ExitStack

import numpy as np

import concourse.bass as bass
from concourse import mybir

F32 = mybir.dt.float32
BF16 = mybir.dt.bfloat16
I32 = mybir.dt.int32
ALU = mybir.AluOpType
ACT = mybir.ActivationFunctionType
X_AXIS = mybir.AxisListType.X

P = 128
NB = 16
NH = NW = 256
NC = 32
NG = 16
GC = NC // NG
NM = 415
KMAX = 16
K1 = KMAX + 1
K0 = 2 * KMAX + 1
NSLOT = K0 * K1
PIX = NH * NW
GROUP = PIX * GC
EPS_GN = 1e-5
EPS_K = 1e-7
EPS_BN = 1e-3
SCALES = (2, 4, 8, 16)
LN2 = float(np.log(2.0))

BAND_FOR = {}
for _r in SCALES:
    if _r == 2:
        _list = [(2, 1, "odd"), (2, 1, "even")]
    else:
        _list = [(_r, 1, "pair"), (_r, 0, "even"), (_r, 0, "odd")]
    for _k in _list:
        BAND_FOR[_k] = len(BAND_FOR)
C_BAND = 0
C_IDENT = C_BAND + P * len(BAND_FOR)
C_ONES = C_IDENT + P
C_BH = C_ONES + P
C_FI = C_BH + 2 * P
C_KEEP = C_FI + NW
C_BF = C_KEEP
C_FB = C_BF + 2 * K0
C_SEL = C_FB + 4 * 4 * K1
C_CEN = C_SEL + 4 * 64
C_PAIR = C_CEN + 64
C_GRP = C_PAIR + 64
C_END = C_GRP + 64


def constants():
    t = np.zeros((P, C_END), np.float64)
    p = np.arange(P)
    for (r, e, src), i in BAND_FOR.items():
        out_row = 2 * p[None, :] + e
        lo, hi = out_row - (r // 2 - 1), out_row + r // 2
        if src == "pair":
            band = (2 * p[:, None] >= lo) & (2 * p[:, None] + 1 <= hi)
        else:
            row = 2 * p[:, None] + (src == "odd")
            band = (row >= lo) & (row <= hi)
        t[:, C_BAND + i * P:C_BAND + (i + 1) * P] = band
    t[:, C_IDENT:C_IDENT + P] = np.eye(P)
    t[:, C_ONES:C_ONES + P] = 1.0
    turn = 2 * np.pi / NH
    k1 = np.arange(K1)
    for q in range(2):
        h = 2 * p + q
        for a in range(1, KMAX + 1):
            t[2 * (a - 1), C_BH + q * P:C_BH + (q + 1) * P] = np.cos(turn * (a * h % NH))
            t[2 * (a - 1) + 1, C_BH + q * P:C_BH + (q + 1) * P] = np.sin(turn * (a * h % NH))
            t[:, C_BF + q * K0 + 2 * a - 1] = np.cos(turn * (a * h % NH))
            t[:, C_BF + q * K0 + 2 * a] = np.sin(turn * (a * h % NH))
        t[K0 - 1, C_BH + q * P:C_BH + (q + 1) * P] = 1.0
        t[:, C_BF + q * K0] = 1.0
    weight = np.where(k1 == 0, 1.0, 2.0) / PIX
    ang = turn * (k1[:, None] * np.arange(NW)[None, :] % NW)
    t[0:K1, C_FI:C_FI + NW] = weight[:, None] * np.cos(ang)
    t[32:32 + K1, C_FI:C_FI + NW] = weight[:, None] * np.sin(ang)
    for v in range(2):
        ang = turn * ((P * v + p)[:, None] * k1[None, :] % NW)
        c, s = np.cos(ang), np.sin(ang)
        at = C_FB + v * 8 * K1
        t[:, at:at + 4 * K1] = np.concatenate([c, -s, c, -s], 1)
        t[:, at + 4 * K1:at + 8 * K1] = np.concatenate([-s, -c, s, c], 1)
    e = np.eye(32)
    for n, sign in enumerate((1.0, -1.0)):
        at = C_SEL + n * 128
        t[0:32, at:at + 32] = e
        t[32:64, at + 32:at + 64] = -e
        t[32:64, at + 64:at + 96] = -sign * e
        t[0:32, at + 96:at + 128] = -sign * e
    pair = np.kron(np.eye(NG), np.full((GC, GC), 1.0 / GC))
    t[0:32, C_CEN:C_CEN + 32] = e - pair
    t[32:64, C_CEN + 32:C_CEN + 64] = e
    t[0:32, C_PAIR:C_PAIR + 32] = pair / PIX
    t[0:32, C_PAIR + 32:C_PAIR + 64] = pair / PIX
    spread = np.kron(np.eye(NG), np.ones((1, GC))) / GROUP
    t[0:NG, C_GRP:C_GRP + 32] = spread
    t[0:NG, C_GRP + 32:C_GRP + 64] = spread
    return t.astype(np.float32)


ENTER = {k: [] for k in range(NG)}
for _g in range(NG):
    ENTER[5 + _g // 2].append(_g)
STATS_AT = 13

LO, HI = 7, 8
WP = NW + LO + HI
SPAN = {2: (-7, 270), 4: (-6, 268), 8: (-4, 264), 16: (0, 256)}
STEP = {4: 1, 8: 2, 16: 4}


def build(nc, x, w_re, w_im, idx0, idx1, gamma, beta, mov_mean, mov_var, table, out):
    ctx = ExitStack()
    with ctx:
        def sb(name, shape, dt=F32):
            return ctx.enter_context(nc.sbuf_tensor(name, shape, dt))

        def sem(name):
            return ctx.enter_context(nc.semaphore(name))

        wtab = nc.dram_tensor("wtab", [NSLOT + 1, 64, 64], F32, kind="Internal").ap()
        vtab = nc.dram_tensor("vtab", [NB, 64, K0 * NC], F32, kind="Internal").ap()

        arena = sb("arena", [P, 2 * 2 * NW * NC])
        cst = sb("cst", [P, C_KEEP])
        ssqb = sb("ssqb", [NG, NB])
        half = NW * NC
        xbuf = [arena[:, n * 2 * half:(n + 1) * 2 * half] for n in range(2)]

        early = ExitStack()
        cst1 = early.enter_context(nc.sbuf_tensor("cst1", [P, C_END - C_KEEP], F32))

        def const(at, rows, cols):
            if at >= C_KEEP:
                return cst1[0:rows, at - C_KEEP:at - C_KEEP + cols]
            return cst[0:rows, at:at + cols]

        def wait(eng, semaphore, count):
            if not isinstance(count, int) or count > 0:
                eng.wait_ge(semaphore, count)

        ident = const(C_IDENT, P, P)
        ones = const(C_ONES, P, P)

        with ExitStack() as one:
            def psum1(name, shape):
                return one.enter_context(nc.psum_tensor(name, shape, F32))

            psz = psum1("psz", [P, 3, 512])
            psx = psum1("psx", [P, 3, 512])
            pss = psum1("pss", [P, 512])
            xh = [arena[:, v * half:(v + 1) * half].rearrange("p (q w c) -> p q w c", q=2, w=P)
                  for v in range(2)]
            at = 2 * half
            modes_all = arena[:, at:at + NSLOT * NB].rearrange("p (s b) -> p s b", b=NB)
            modes = modes_all[0:64]
            at += NSLOT * NB
            zsb = arena[:, at:at + 2 * K0 * NC].rearrange("p (v k c) -> p v k c", v=2, k=K0)
            at += 2 * K0 * NC
            wrow = arena[0:83, 4 * half - 4096:4 * half].rearrange("p (i o) -> p i o", i=64)
            assert at <= 4 * half - 4096
            NJ = 4
            junk1 = one.enter_context(nc.sbuf_tensor("junk1", [P, 2, NJ, 512], BF16))
            ssq1 = one.enter_context(nc.sbuf_tensor("ssq1", [P, 2, NG], F32))
            zero = one.enter_context(nc.sbuf_tensor("zero", [P, 4096], F32))
            wraw = one.enter_context(nc.sbuf_tensor("wraw", [83, 2, 5, NC * NC], F32))
            idx = one.enter_context(nc.sbuf_tensor("idx", [83, 2, 5], I32))
            sl = one.enter_context(nc.sbuf_tensor("sl", [83, 6, 5], F32))
            slot = one.enter_context(nc.sbuf_tensor("slot", [83, 5], I32))

            s_cst = sem("consts_in")
            s_xin = [sem(f"x_half_in{v}") for v in range(2)]
            s_xsq = [sem(f"x_half_squared{v}") for v in range(2)]
            s_z = [[sem(f"rows_done{v}_{k}") for k in range(3)] for v in range(2)]
            s_ze = [sem(f"rows_kept{k}") for k in range(3)]
            s_m = [sem(f"modes_done{k}") for k in range(3)]
            s_me = [sem(f"modes_kept{k}") for k in range(3)]
            s_ss = sem("squares_summed")
            s_sse = sem("squares_kept")
            s_idx = sem("indices_in")
            s_sl = sem("slot_steps")
            s_zero = sem("zero_set")
            s_clear = sem("table_cleared")
            s_wrow = sem("weight_rows_built")
            s_wraw = sem("weights_raw_in")
            s_scat = sem("weight_rows_out")
            s_mzero = sem("mode_zeros_set")

            ZC = [(0, 11), (11, 11), (22, 10)]
            XA = [(0, 15), (15, 14), (29, 4)]
            xv = x.rearrange("b (p q) (v w) c -> b v p q (w c)", q=2, v=2)

            with nc.Block() as block:
                @block.sync
                def _(sync):
                    sync.dma_start(cst[:, :], table[:, 0:C_KEEP]).then_inc(s_cst, 16)
                    sync.dma_start(cst1[:, :], table[:, C_KEEP:C_END]).then_inc(s_cst, 16)

                    def load(n):
                        for v in range(2):
                            wait(sync, s_xsq[v], n * NG)
                            wait(sync, s_z[v][2], n)
                            sync.dma_start(xh[v].rearrange("p q w c -> p q (w c)"),
                                           xv[bass.ds(n, 1), v].rearrange("b p q m -> (b p) q m"))\
                                .then_inc(s_xin[v], 16)

                    load(0)
                    with sync.Fori(1, NB) as n:
                        load(n)

                @block.gpsimd
                def _(pool):
                    pool.memset(zero[:, :], 0.0).then_inc(s_zero, 1)
                    pool.dma_start(idx[:, 0, :], idx0.rearrange("(p t) -> p t", p=83)).then_inc(s_idx, 16)
                    pool.dma_start(idx[:, 1, :], idx1.rearrange("(p t) -> p t", p=83)).then_inc(s_idx, 16)
                    for j, w in enumerate((w_re, w_im)):
                        pool.dma_start(wraw[:, j], w.rearrange("(p t) i o -> p t (i o)", p=83)).then_inc(s_wraw, 16)
                    pool.wait_ge(s_zero, 1)
                    flat = wtab.rearrange("s i o -> s (i o)")
                    done = 0
                    while done < NSLOT + 1:
                        k = min(P, NSLOT + 1 - done)
                        pool.dma_start(flat[done:done + k, :], zero[0:k, :]).then_inc(s_clear, 16)
                        done += k
                    pool.wait_ge(s_clear, 16 * 5)
                    pool.wait_ge(s_sl, SLOT_STEPS)
                    pool.wait_ge(s_wraw, 32)
                    for t in range(5):
                        if t:
                            pool.wait_ge(s_scat, 16 * t)
                        re, im = (wraw[:, j, t, :].rearrange("p (i o) -> p i o", i=NC) for j in range(2))
                        pool.tensor_copy(wrow[:, 0:32, 0:32], re).then_inc(s_wrow, 1)
                        pool.tensor_copy(wrow[:, 0:32, 32:64], im).then_inc(s_wrow, 1)
                        pool.tensor_copy(wrow[:, 32:64, 32:64], re).then_inc(s_wrow, 1)
                        pool.tensor_scalar(wrow[:, 32:64, 0:32], im, -1.0, None, ALU.mult).then_inc(s_wrow, 1)
                        pool.wait_ge(s_wrow, 4 * (t + 1))
                        pool.indirect_dma_start(
                            flat, bass.IndirectOffsetOnAxis(ap=slot[:, t:t + 1], axis=0),
                            wrow.rearrange("p i o -> p (i o)"), None).then_inc(s_scat, 16)
                    pool.wait_ge(s_scat, 16 * 5)

                @block.scalar
                def _(act):
                    def squares(n):
                        for v in range(2):
                            act.wait_ge(s_xin[v], n * 16 + 16)
                            if v == 0:
                                wait(act, s_ss, n)
                            for g in range(NG):
                                wait(act, s_xsq[v], n * NG + max(g - NJ + 1, 0))
                                nc.scalar.activation(
                                    junk1[:, v, g % NJ, :].rearrange("p (w c) -> p w c", c=GC),
                                    xh[v].rearrange("p q w c -> p (q w) c")[:, :, GC * g:GC * (g + 1)],
                                    ACT.Square, accum_out=ssq1[:, v, g:g + 1]).then_inc(s_xsq[v], 1)

                    squares(0)
                    with act.Fori(1, NB) as n:
                        squares(n)

                @block.vector
                def _(dve):
                    nc.vector.memset(modes_all[64:128], 0.0).then_inc(s_mzero, 1)
                    steps = [0]

                    def link(ins):
                        steps[0] += 1
                        ins.then_inc(s_sl, 1)
                        dve.wait_ge(s_sl, steps[0])

                    dve.wait_ge(s_idx, 32)
                    k0, k1, hi, t0, t1, t2 = (sl[:, j, :] for j in range(6))
                    link(nc.vector.tensor_copy(k0, idx[:, 0, :]))
                    link(nc.vector.tensor_copy(k1, idx[:, 1, :]))
                    link(nc.vector.tensor_scalar(hi, k0, float(NH // 2), -float(NH), ALU.is_ge, ALU.mult))
                    link(nc.vector.tensor_tensor(k0, k0, hi, ALU.add))
                    link(nc.vector.tensor_scalar(hi, k0, 0.0, None, ALU.is_gt))
                    link(nc.vector.tensor_scalar(t0, k0, -1.0, None, ALU.mult))
                    link(nc.vector.tensor_tensor(t0, k0, t0, ALU.max))
                    link(nc.vector.tensor_tensor(t1, t0, k1, ALU.max))
                    link(nc.vector.tensor_scalar(t1, t1, float(KMAX), float(2 * NSLOT), ALU.is_gt, ALU.mult))
                    link(nc.vector.scalar_tensor_tensor(t2, t0, 2.0, hi, ALU.mult, ALU.subtract))
                    link(nc.vector.scalar_tensor_tensor(t2, t2, float(K1), k1, ALU.mult, ALU.add))
                    link(nc.vector.tensor_tensor(t2, t2, t1, ALU.add))
                    link(nc.vector.tensor_scalar(t2, t2, float(NSLOT), None, ALU.min))
                    link(nc.vector.tensor_copy(slot[:, :], t2))
                    assert steps[0] == SLOT_STEPS

                    def keep(n):
                        wait(dve, s_m[2], n)
                        for v in range(2):
                            for k, (c0, m) in enumerate(ZC):
                                dve.wait_ge(s_z[v][k], n + 1)
                                nc.vector.tensor_copy(
                                    zsb[:, v, :, c0:c0 + m].rearrange("p k c -> p c k"),
                                    psz[:, k, 0:m * K0].rearrange("p (c k) -> p c k", c=m))\
                                    .then_inc(s_ze[k], 1)
                        for k, (j0, m) in enumerate(XA):
                            dve.wait_ge(s_m[k], n + 1)
                            for ri in range(2):
                                src = psx[0:32, k, 0:m * 2 * K1].rearrange(
                                    "p (j r f) -> p j r f", j=m, r=2)[:, :, ri, :]
                                dst = modes[32 * ri:32 * ri + 32, j0 * K1:(j0 + m) * K1, bass.ds(n, 1)]\
                                    .rearrange("p (j f) b -> p j (f b)", j=m)
                                last = nc.vector.tensor_copy(dst, src)
                            last.then_inc(s_me[k], 1)
                        dve.wait_ge(s_ss, n + 1)
                        nc.vector.tensor_copy(ssqb[:, bass.ds(n, 1)], pss[0:NG, 0:1]).then_inc(s_sse, 1)

                    keep(0)
                    with dve.Fori(1, NB) as n:
                        keep(n)

                @block.tensor
                def _(pe):
                    pe.wait_ge(s_cst, 32)
                    def transform(n):
                        for v in range(2):
                            pe.wait_ge(s_xin[v], n * 16 + 16)
                            for k, (c0, m) in enumerate(ZC):
                                wait(pe, s_ze[k], n * 2 + v)
                                for c in range(m):
                                    for q in range(2):
                                        last = nc.tensor.matmul(
                                            psz[:, k, c * K0:(c + 1) * K0], xh[v][:, q, :, c0 + c],
                                            const(C_BF + q * K0, P, K0), start=(q == 0), stop=(q == 1))
                                last.then_inc(s_z[v][k], 1)
                        for k in range(3):
                            pe.wait_ge(s_ze[k], n * 2 + 2)
                        for k, (j0, m) in enumerate(XA):
                            wait(pe, s_me[k], n)
                            j = j0
                            while j < j0 + m:
                                cols = (4 if j else 2) * K1
                                comps = [(0, 0)] if j == 0 else [(j, 0), (j + 1, 1)]
                                ops = [(v, comp, kind) for comp, kind in comps for v in range(2)]
                                for i, (v, comp, kind) in enumerate(ops):
                                    last = nc.tensor.matmul(
                                        psx[0:32, k, (j - j0) * 2 * K1:(j - j0) * 2 * K1 + cols],
                                        zsb[:, v, comp, :],
                                        const(C_FB + v * 8 * K1 + kind * 4 * K1, P, cols),
                                        start=(i == 0), stop=(i == len(ops) - 1))
                                j += 2 if j else 1
                            last.then_inc(s_m[k], 1)
                        for v in range(2):
                            pe.wait_ge(s_xsq[v], n * NG + NG)
                        wait(pe, s_sse, n)
                        for v in range(2):
                            last = nc.tensor.matmul(pss[0:NG, 0:1], ssq1[:, v, :], ones[:, 0:1],
                                                    start=(v == 0), stop=(v == 1))
                        last.then_inc(s_ss, 1)

                    transform(0)
                    with pe.Fori(1, NB) as n:
                        transform(n)

        with ExitStack() as mid:
            def psum2(name, shape):
                return mid.enter_context(nc.psum_tensor(name, shape, F32))

            psy = psum2("psymix", [P, 3, 512])
            psv = psum2("psv", [P, 5, 512])
            ymodes = arena[0:64, 0:NSLOT * NB].rearrange("p (s b) -> p s b", b=NB)
            at = NSLOT * NB
            NWT = 3
            wt = [arena[:, at + j * K1 * 64:at + (j + 1) * K1 * 64].rearrange("p (s o) -> p s o", s=K1)
                  for j in range(NWT)]
            wt_low = arena[64:128, at:at + NWT * K1 * 64]
            at += NWT * K1 * 64
            assert at <= 2 * half
            at = 2 * half + NSLOT * NB
            yb = arena[:, at:at + NSLOT]
            at += NSLOT + 15
            vsb = arena[0:64, at:at + K0 * NC].rearrange("p (k c) -> p k c", c=NC)
            st = mid.enter_context(nc.sbuf_tensor("st", [64, 6, NB], F32))

            s_st = sem("stat_matmuls")
            s_stv = sem("stat_steps")
            s_sta = sem("stat_logs")
            s_wt = [sem(f"weights_in{j}") for j in range(NWT)]
            s_mix = [sem(f"mixed{j}") for j in range(NWT)]
            s_mixe = [sem(f"mixed_kept{j}") for j in range(NWT)]
            s_yb = sem("sample_modes_picked")
            s_v = sem("parts_done")
            s_ve = sem("parts_kept")
            s_vout = sem("parts_out")
            s_vz = sem("parts_zeroed")

            with nc.Block() as block:
                @block.sync
                def _(sync):
                    def load(i):
                        for j in range(NWT):
                            wait(sync, s_mix[j], i)
                            sync.dma_start(
                                wt[j][0:64], wtab[bass.ds(i * (NWT * K1) + j * K1, K1)].rearrange("s i o -> i s o"))\
                                .then_inc(s_wt[j], 16)

                    load(0)
                    with sync.Fori(1, K0 // NWT) as i:
                        load(i)
                    with sync.Fori(0, NB) as n:
                        sync.wait_ge(s_ve, n + 1)
                        sync.dma_start(vtab[bass.ds(n, 1)].rearrange("b p m -> (b p) m"),
                                       vsb.rearrange("p k c -> p (k c)")).then_inc(s_vout, 16)
                    sync.wait_ge(s_vout, 16 * NB)

                @block.scalar
                def _(act):
                    act.wait_ge(s_stv, 4)
                    nc.scalar.activation(st[:, 2, :], st[:, 1, :], ACT.Ln).then_inc(s_sta, 1)
                    act.wait_ge(s_sta, 1)
                    nc.scalar.activation(st[:, 2, :], st[:, 2, :], ACT.Exp, scale=-0.5).then_inc(s_sta, 1)

                @block.vector
                def _(dve):
                    steps = [0]

                    def link(ins):
                        steps[0] += 1
                        ins.then_inc(s_stv, 1)
                        dve.wait_ge(s_stv, steps[0])

                    nc.vector.memset(vsb, 0.0).then_inc(s_vz, 1)
                    nc.vector.memset(yb[64:128], 0.0).then_inc(s_vz, 1)
                    nc.vector.memset(wt_low, 0.0).then_inc(s_vz, 1)
                    dve.wait_ge(s_st, 1)
                    link(nc.vector.tensor_copy(st[:, 0, :], psy[0:64, 0, 0:NB]))
                    link(nc.vector.tensor_tensor(st[:, 0, :], st[:, 0, :], st[:, 0, :], ALU.mult))
                    link(nc.vector.tensor_tensor(st[:, 1, :], psy[0:64, 1, 0:NB], st[:, 0, :], ALU.subtract))
                    link(nc.vector.tensor_scalar(st[:, 1, :], st[:, 1, :], 0.0, EPS_GN, ALU.max, ALU.add))
                    dve.wait_ge(s_sta, 2)
                    link(nc.vector.tensor_tensor(st[:, 3, :], st[:, 2, :], st[:, 2, :], ALU.mult))
                    link(nc.vector.tensor_tensor(st[:, 3, :], st[:, 3, :], st[:, 1, :], ALU.mult))
                    link(nc.vector.tensor_scalar(st[:, 3, :], st[:, 3, :], -0.5, 1.5, ALU.mult, ALU.add))
                    link(nc.vector.tensor_tensor(st[:, 4, :], st[:, 3, :], st[:, 2, :], ALU.mult))
                    link(nc.vector.tensor_copy(modes[:, 0, :], psy[0:64, 2, 0:NB]))
                    link(nc.vector.tensor_tensor(
                        modes, modes, st[:, 4:5, :].broadcast_to([64, NSLOT, NB]), ALU.mult))
                    with dve.Fori(0, K0 // NWT) as i:
                        for j in range(NWT):
                            dve.wait_ge(s_mix[j], i + 1)
                            nc.vector.tensor_copy(
                                ymodes[:, bass.ds(i * (NWT * K1) + j * K1, K1), :],
                                psy[0:64, j, 0:K1 * NB].rearrange("p (s b) -> p s b", b=NB))\
                                .then_inc(s_mixe[j], 1)
                    for j in range(NWT):
                        dve.wait_ge(s_mixe[j], K0 // NWT)
                    dve.wait_ge(s_vz, 3)
                    def parts(n):
                        wait(dve, s_v, n)
                        nc.vector.tensor_copy(yb[0:64], ymodes[:, :, bass.ds(n, 1)].rearrange("p s b -> p (s b)"))\
                            .then_inc(s_yb, 1)
                        dve.wait_ge(s_v, n + 1)
                        wait(dve, s_vout, n * 16)
                        for r in range(2):
                            nc.vector.tensor_copy(
                                vsb[32 * r:32 * r + K1, 0:K0 - 1, :],
                                psv[0:K1, 0:4, :].rearrange("p b (k r c) -> p (b k) r c", r=2, c=NC)[:, :, r, :])
                            last = nc.vector.tensor_copy(vsb[32 * r:32 * r + K1, K0 - 1, :],
                                                         psv[0:K1, 4, r * NC:(r + 1) * NC])
                        last.then_inc(s_ve, 1)

                    parts(0)
                    with dve.Fori(1, NB) as n:
                        parts(n)

                @block.tensor
                def _(pe):
                    nc.tensor.matmul(psy[0:64, 0, 0:NB], const(C_PAIR, 64, 64), modes[:, 0, :],
                                     start=True, stop=True)
                    nc.tensor.matmul(psy[0:64, 1, 0:NB], const(C_GRP, NG, 64), ssqb[:, :],
                                     start=True, stop=True)
                    nc.tensor.matmul(psy[0:64, 2, 0:NB], const(C_CEN, 64, 64), modes[:, 0, :],
                                     start=True, stop=True).then_inc(s_st, 1)
                    pe.wait_ge(s_stv, MID_STEPS)
                    pe.wait_ge(s_vz, 3)
                    def mix(i):
                        for j in range(NWT):
                            pe.wait_ge(s_wt[j], i * 16 + 16)
                            wait(pe, s_mixe[j], i)
                            for s in range(K1):
                                last = nc.tensor.matmul(
                                    psy[0:64, j, s * NB:(s + 1) * NB], wt[j][:, s, :],
                                    modes_all[:, bass.ds(i * (NWT * K1) + (j * K1 + s), 1), :]
                                    .rearrange("p s b -> p (s b)"), start=True, stop=True)
                            last.then_inc(s_mix[j], 1)

                    mix(0)
                    with pe.Fori(1, K0 // NWT) as i:
                        mix(i)

                    def parts(n):
                        pe.wait_ge(s_yb, n + 1)
                        wait(pe, s_ve, n)
                        nc.tensor.matmul(psv[0:K1, 4, 0:64], yb[:, 0:K1], const(C_SEL, P, 64),
                                         start=True, stop=True)
                        for a in range(1, KMAX + 1):
                            col = 128 * (a - 1)
                            for s in range(2):
                                j = 2 * a - 1 + s
                                last = nc.tensor.matmul(
                                    psv[0:K1, col // 512, col % 512:col % 512 + 128],
                                    yb[:, j * K1:(j + 1) * K1], const(C_SEL + 128 * s, P, 128),
                                    start=(s == 0), stop=(s == 1))
                        last.then_inc(s_v, 1)

                    parts(0)
                    with pe.Fori(1, NB) as n:
                        parts(n)

        early.close()
        with ExitStack() as two:
            def sb2(name, shape, dt=F32):
                return two.enter_context(nc.sbuf_tensor(name, shape, dt))

            def psum3(name, shape):
                return two.enter_context(nc.psum_tensor(name, shape, F32))

            NPX = NW * GC
            vin = sb2("vin", [P, K0, NC])
            usb = [sb2(f"usb{i}", [K0, NPX]) for i in range(2)]
            xn = sb2("xn", [P, 2, WP * GC])
            wsum = {2: [sb2(f"w2_{i}", [P, 2, WP * GC]) for i in range(2)],
                    4: [sb2(f"w4_{i}", [P, 2, WP * GC]) for i in range(2)]}
            wsum[8] = [sb2("w8", [P, 2, WP * GC])] * 2
            wsum[16] = [sb2("w16", [P, 2, NPX])] * 2
            pair = {r: sb2(f"pair{r}", [P, NPX]) for r in SCALES}
            logs = {2: [sb2("log2", [P, 2 * NPX])] * 2,
                    4: [sb2("log4", [P, 2 * NPX])] * 2,
                    8: [sb2(f"log8_{i}", [P, 2 * NPX]) for i in range(2)],
                    16: [sb2("log16", [P, 2 * NPX])] * 2}
            junk = sb2("junk", [P, 2 * NPX], BF16)
            stat = sb2("stat", [P, 4 * NG])
            red = sb2("red", [32, 2])
            diag = sb2("diag", [32, 64])
            sm = sb2("sm", [P, 8, NG])
            sc1 = sb2("sc1", [P, 4])
            aff = sb2("aff", [P, 2, 2, NG])
            par = sb2("par", [P, 2, NC])
            raw = sm[:, :, :].rearrange("p a g -> p (a g)").rearrange("p (j c) -> p j c", c=NC)
            eps_k = sb2("eps_k", [P, 1])[:, :]

            psu = psum3("psu", [P, 512])
            psy = psum3("psy", [P, 2, 512])
            psm = [psum3(f"psm{i}", [P, 2, 512]) for i in range(2)]
            pst = psum3("pst", [P, 512])

            s_par = sem("params_in")
            s_pv = sem("param_steps")
            s_pa = sem("param_logs")
            s_x = [sem(f"x_in{i}") for i in range(2)]
            s_out = [sem(f"out_stored{i}") for i in range(2)]
            s_vin = sem("parts_in")
            s_u = sem("columns_done")
            s_us = sem("columns_kept")
            s_y = sem("y_done")
            s_x1 = sem("x1_done")
            s_mm = sem("min_max_done")
            s_sq = sem("x1_squared")
            s_t1 = sem("stat_sums_done")
            s_t2 = sem("extrema_spread")
            s_tv = sem("stat2_steps")
            s_ta = sem("stat2_logs")
            s_xn = sem("scaled_ready")
            s_pad = sem("pads_zeroed")
            s_w = {r: sem(f"row_sums{r}_ready") for r in SCALES}
            s_pr = {r: sem(f"pair{r}_ready") for r in SCALES}
            s_ms = {r: sem(f"measure{r}_done") for r in SCALES}
            s_l = {r: sem(f"log{r}_ready") for r in SCALES}
            s_t = sem("log4_plus_3_log2_ready")
            s_lo = sem("lower_logs_taken_off_log8")
            s_f = sem("exponent_ready")
            s_xd = sem("x1_shifted")
            s_o = sem("outputs_done")

            xs = x.rearrange("b (p q) w c -> b p (q w c)", q=2)
            os_ = out.rearrange("b (p q) w c -> b p (q w c)", q=2)

            def group(par_, g):
                return xbuf[par_].rearrange("p (m c) -> p m c", c=NC)[:, :, GC * g:GC * (g + 1)]

            def as2(ap):
                return ap.rearrange("p (m c) -> p m c", c=GC)

            def cols(ap, w0, m):
                if ap.shape[-1] == NPX:
                    return ap[:, :, w0 * GC:(w0 + m) * GC]
                return ap[:, :, (w0 + LO) * GC:(w0 + LO + m) * GC]

            def walk(eng, enter, prepare, step, stats, finish=None):
                def sample(n, par_):
                    last = isinstance(n, int) and n == NB - 1
                    for k in range(NG):
                        entering = [] if last else [(n + 1, 1 - par_, g) for g in ENTER[k]]
                        after = (n, par_, k + 1) if k + 1 < NG else None if last else (n + 1, 1 - par_, 0)
                        before = (n, par_, k - 1) if k else None if isinstance(n, int) and n == 0 else \
                            (n - 1, 1 - par_, NG - 1)
                        step(n, par_, k, entering, before, after)
                        if not last and k in (STATS_AT, STATS_AT + 1):
                            stats(n + 1, 1 - par_, k - STATS_AT)

                for g in range(NG):
                    enter(0, 0, g)
                stats(0, 0, 0)
                stats(0, 0, 1)
                prepare(0, 0, 0)
                sample(0, 0)
                with eng.Fori(0, NB // 2 - 1) as two_samples:
                    sample(two_samples * 2 + 1, 1)
                    sample(two_samples * 2 + 2, 0)
                sample(NB - 1, 1)
                if finish:
                    finish(NB - 1, 1, NG - 1)

            with nc.Block() as block:
                @block.sync
                def _(sync):
                    for j, p_ in enumerate((gamma, beta, mov_mean, mov_var)):
                        sync.dma_start(raw[:, j, :], p_.rearrange("(a c) -> a c", a=1).broadcast_to([P, NC]))\
                            .then_inc(s_par, 16)

                    def load(n, par_):
                        sync.dma_start(xbuf[par_], xs[bass.ds(n, 1)].rearrange("b p m -> (b p) m"))\
                            .then_inc(s_x[par_], 16)

                    def load_parts(n):
                        wait(sync, s_u, n * NG)
                        sync.dma_start(vin[0:64, :, :].rearrange("p k c -> p (k c)"),
                                       vtab[bass.ds(n, 1)].rearrange("b p m -> (b p) m"))\
                            .then_inc(s_vin, 16)

                    def store(n, par_):
                        sync.wait_ge(s_o, n * NG + NG)
                        sync.dma_start(os_[bass.ds(n, 1)].rearrange("b p m -> (b p) m"), xbuf[par_])\
                            .then_inc(s_out[par_], 16)

                    def turn(n, par_):
                        store(n, par_)
                        sync.wait_ge(s_out[par_], n * 8 + (16 - 8 * par_))
                        load(n + 2, par_)
                        load_parts(n + 2)

                    load_parts(0)
                    load(0, 0)
                    load(1, 1)
                    load_parts(1)
                    turn(0, 0)
                    with sync.Fori(0, NB // 2 - 2) as two_samples:
                        turn(two_samples * 2 + 1, 1)
                        turn(two_samples * 2 + 2, 0)
                    turn(NB - 3, 1)
                    store(NB - 2, 0)
                    store(NB - 1, 1)
                    for par_ in range(2):
                        sync.wait_ge(s_out[par_], 16 * NB // 2)

                @block.tensor
                def _(pe):
                    pe.wait_ge(s_pad, 3)

                    def columns(n, par_, g):
                        if g == 0:
                            pe.wait_ge(s_vin, n * 16 + 16)
                        wait(pe, s_us, n * NG + g)
                        for c in range(GC):
                            last = nc.tensor.matmul(psu[0:K0, c * NW:(c + 1) * NW],
                                                    vin[:, :, GC * g + c],
                                                    const(C_FI, P, NW), start=True, stop=True)
                        last.then_inc(s_u, 1)

                    def rows(n, par_, g):
                        pe.wait_ge(s_us, n * NG + (g + 1))
                        wait(pe, s_x1, n * NG + g)
                        for q in range(2):
                            last = nc.tensor.matmul(psy[:, q, :], const(C_BH + q * P, K0, P), usb[g % 2][:, :],
                                                    start=True, stop=True)
                        last.then_inc(s_y, 1)

                    def enter(n, par_, g):
                        columns(n, par_, g)
                        rows(n, par_, g)

                    def stats(n, par_, part):
                        if part:
                            pe.wait_ge(s_tv, n * STAT_STEPS + 6)
                            nc.tensor.matmul(pst[:, 256:320], ones[0:32, :], diag[:, :],
                                             start=True, stop=True).then_inc(s_t2, 1)
                            return
                        wait(pe, s_tv, n * STAT_STEPS)
                        pe.wait_ge(s_mm, n * NG + NG)
                        pe.wait_ge(s_sq, n * NG + NG)
                        nc.tensor.matmul(pst[:, 0:32], ones, stat[:, 0:32], start=True, stop=True)
                        nc.tensor.matmul(pst[0:32, 128:256], stat[:, 32:64], ident, start=True, stop=True)\
                            .then_inc(s_t1, 1)

                    def measure(n, k, r):
                        w = wsum[r][k % 2]
                        dst = psm[SCALES.index(r) % 2]
                        band = {key[1:]: const(C_BAND + v * P, P, P) for key, v in BAND_FOR.items() if key[0] == r}
                        rhs = {"even": cols(w, 0, NW)[:, 0, :], "odd": cols(w, 0, NW)[:, 1, :],
                               "pair": pair[r][:, :]}
                        c = n * NG + k
                        pe.wait_ge(s_w[r], c + 1)
                        before = {2: (8, 0), 4: (16, 0), 8: (2, 1), 16: (4, 1)}[r]
                        wait(pe, s_l[before[0]], c + before[1])
                        for e in (0, 1):
                            keys = [key for key in band if key[0] == e]
                            if e == 1 and r > 2:
                                pe.wait_ge(s_pr[r], c + 1)
                            for j, key in enumerate(keys):
                                last = nc.tensor.matmul(dst[:, e, :], band[key], rhs[key[1]],
                                                        start=(j == 0), stop=(j == len(keys) - 1))
                        last.then_inc(s_ms[r], 1)

                    def step(n, par_, k, entering, before, after):
                        if entering:
                            columns(*entering[0])
                        measure(n, k, 2)
                        if entering:
                            rows(*entering[0])
                        measure(n, k, 4)
                        if len(entering) > 1:
                            columns(*entering[1])
                        measure(n, k, 8)
                        if len(entering) > 1:
                            rows(*entering[1])
                        measure(n, k, 16)

                    walk(pe, enter, lambda *a: None, step, stats)

                @block.scalar
                def _(act):
                    act.wait_ge(s_pv, 1)
                    nc.scalar.activation(par[:, 0, :], raw[:, 3, :], ACT.Ln).then_inc(s_pa, 1)
                    act.wait_ge(s_pa, 1)
                    nc.scalar.activation(par[:, 0, :], par[:, 0, :], ACT.Exp, scale=-0.5).then_inc(s_pa, 1)
                    act.wait_ge(s_pad, 3)

                    def keep(n, par_, g):
                        act.wait_ge(s_u, n * NG + (g + 1))
                        wait(act, s_y, n * NG + (g - 1))
                        nc.scalar.activation(usb[g % 2][:, :].rearrange("p (w c) -> p c w", c=GC),
                                             psu[0:K0, :].rearrange("p (c w) -> p c w", c=GC),
                                             ACT.Copy).then_inc(s_us, 1)

                    def square(n, par_, g):
                        act.wait_ge(s_x1, n * NG + (g + 1))
                        if g == 0:
                            wait(act, s_t1, n)
                        wait(act, s_sq, n * NG + g)
                        nc.scalar.activation(as2(junk[:, :]), group(par_, g), ACT.Square,
                                             accum_out=stat[:, NG + g:NG + g + 1]).then_inc(s_sq, 1)

                    def enter(n, par_, g):
                        keep(n, par_, g)
                        square(n, par_, g)

                    def stats(n, par_, part):
                        if part:
                            return
                        act.wait_ge(s_tv, n * STAT_STEPS + 9)
                        nc.scalar.activation(sm[:, 4, :], sm[:, 3, :], ACT.Ln).then_inc(s_ta, 1)
                        act.wait_ge(s_ta, n * 2 + 1)
                        nc.scalar.activation(sm[:, 4, :], sm[:, 4, :], ACT.Exp, scale=-0.5).then_inc(s_ta, 1)

                    def scaled(n, par_, k):
                        if k == 0:
                            act.wait_ge(s_tv, n * STAT_STEPS + STAT_STEPS)
                        wait(act, s_w[2], n * NG + k)
                        nc.scalar.activation(
                            cols(xn, 0, NW).rearrange("p q (w c) -> p q w c", c=GC),
                            group(par_, k).rearrange("p (q w) c -> p q w c", q=2),
                            ACT.Relu, scale=aff[:, par_, 0, k:k + 1], bias=aff[:, par_, 1, k:k + 1])\
                            .then_inc(s_xn, 1)

                    def log(n, par_, k, r):
                        dst = logs[r][k % 2]
                        c = n * NG + k
                        if r == 2:
                            wait(act, s_lo, c)
                        elif r == 4:
                            wait(act, s_t, c)
                        elif r == 8:
                            wait(act, s_o, c - 1)
                        else:
                            wait(act, s_f, c)
                        if r == 2:
                            act.wait_ge(s_pr[2], c + 1)
                            nc.scalar.activation(dst[:, 0:NPX], pair[2][:, :], ACT.Ln, bias=eps_k)
                            act.wait_ge(s_ms[2], c + 1)
                            nc.scalar.activation(dst[:, NPX:2 * NPX], psm[0][:, 1, :], ACT.Ln,
                                                 bias=eps_k).then_inc(s_l[2], 1)
                        else:
                            act.wait_ge(s_ms[r], c + 1)
                            nc.scalar.activation(
                                dst[:, :], psm[SCALES.index(r) % 2][:, :, :].rearrange("p e m -> p (e m)"),
                                ACT.Ln, bias=eps_k).then_inc(s_l[r], 1)

                    def step(n, par_, k, entering, before, after):
                        if before:
                            log(*before, 16)
                        if after:
                            scaled(*after)
                        if entering:
                            keep(*entering[0])
                        log(n, par_, k, 2)
                        if entering:
                            square(*entering[0])
                        log(n, par_, k, 4)
                        if len(entering) > 1:
                            keep(*entering[1])
                        log(n, par_, k, 8)
                        if len(entering) > 1:
                            square(*entering[1])

                    walk(act, enter, scaled, step, stats, lambda *a: log(*a, 16))

                @block.vector
                def _(dve):
                    steps = [0]

                    def plink(ins):
                        steps[0] += 1
                        ins.then_inc(s_pv, 1)
                        dve.wait_ge(s_pv, steps[0])

                    nc.vector.memset(eps_k, EPS_K).then_inc(s_pad, 1)
                    nc.vector.memset(xn[:, :, :], 0.0).then_inc(s_pad, 1)
                    nc.vector.memset(vin[64:128, :, :], 0.0).then_inc(s_pad, 1)
                    dve.wait_ge(s_par, 64)
                    ga, be, mm_, va = (raw[:, j, :] for j in range(4))
                    kc, dc = par[:, 0, :], par[:, 1, :]
                    plink(nc.vector.tensor_scalar(va, va, EPS_BN, None, ALU.add))
                    dve.wait_ge(s_pa, 2)
                    plink(nc.vector.tensor_tensor(dc, kc, kc, ALU.mult))
                    plink(nc.vector.tensor_tensor(dc, dc, va, ALU.mult))
                    plink(nc.vector.tensor_scalar(dc, dc, -0.5, 1.5, ALU.mult, ALU.add))
                    plink(nc.vector.tensor_tensor(kc, kc, dc, ALU.mult))
                    plink(nc.vector.tensor_tensor(kc, kc, ga, ALU.mult))
                    plink(nc.vector.tensor_tensor(dc, kc, mm_, ALU.mult))
                    plink(nc.vector.tensor_tensor(dc, be, dc, ALU.subtract))
                    plink(nc.vector.tensor_scalar(kc, kc, 1.0 / (10.0 * LN2), None, ALU.mult))
                    assert steps[0] == PARAM_STEPS

                    def add(n, par_, g):
                        if g == 0:
                            dve.wait_ge(s_x[par_], n * 8 + (16 - 8 * par_))
                            wait(dve, s_t1, n)
                        dve.wait_ge(s_y, n * NG + (g + 1))
                        nc.vector.scalar_tensor_tensor(
                            group(par_, g), group(par_, g), 1.0,
                            as2(psy[:, :, :].rearrange("p q m -> p (q m)")), ALU.mult, ALU.add,
                            accum_out=stat[:, g:g + 1]).then_inc(s_x1, 1)

                    def extrema(n, par_, g):
                        dve.wait_ge(s_x1, n * NG + (g + 1))
                        for j, op in ((2, ALU.min), (3, ALU.max)):
                            last = nc.vector.tensor_reduce(stat[:, j * NG + g:j * NG + g + 1],
                                                           group(par_, g), mybir.AxisListType.XY, op)
                        last.then_inc(s_mm, 1)

                    def enter(n, par_, g):
                        add(n, par_, g)
                        extrema(n, par_, g)

                    def stats(n, par_, part):
                        k = [13 * part]

                        def link(ins):
                            k[0] += 1
                            ins.then_inc(s_tv, 1)
                            dve.wait_ge(s_tv, n * STAT_STEPS + k[0])

                        mean, ex2, t, ve, r0, s, lo, hi = (sm[:, j, :] for j in range(8))
                        if part:
                            stats_end(n, par_, link, mean, t, s, lo, hi)
                            assert k[0] == STAT_STEPS, k[0]
                            return
                        dve.wait_ge(s_t1, n + 1)
                        ext = pst[0:32, 128:256]
                        link(nc.vector.tensor_reduce(red[:, 0:1], ext, X_AXIS, ALU.min))
                        link(nc.vector.tensor_reduce(red[:, 1:2], ext, X_AXIS, ALU.max))
                        for j in range(2):
                            link(nc.vector.tensor_scalar(diag[:, 32 * j:32 * j + 32], ident[0:32, 0:32],
                                                         red[:, j:j + 1], None, ALU.mult))
                        link(nc.vector.tensor_scalar(mean, pst[:, 0:16], 1.0 / GROUP, None, ALU.mult))
                        link(nc.vector.tensor_scalar(ex2, pst[:, 16:32], 1.0 / GROUP, None, ALU.mult))
                        link(nc.vector.tensor_tensor(t, mean, mean, ALU.mult))
                        link(nc.vector.tensor_tensor(ve, ex2, t, ALU.subtract))
                        link(nc.vector.tensor_scalar(ve, ve, 0.0, EPS_GN, ALU.max, ALU.add))
                        dve.wait_ge(s_ta, n * 2 + 2)
                        link(nc.vector.tensor_tensor(t, r0, r0, ALU.mult))
                        link(nc.vector.tensor_tensor(t, t, ve, ALU.mult))
                        link(nc.vector.tensor_scalar(t, t, -0.5, 1.5, ALU.mult, ALU.add))
                        link(nc.vector.tensor_tensor(s, r0, t, ALU.mult))
                        assert k[0] == 13, k[0]

                    def stats_end(n, par_, link, mean, t, s, lo, hi):
                        dve.wait_ge(s_t2, n + 1)
                        link(nc.vector.tensor_tensor(lo, pst[:, 256:272], mean, ALU.subtract))
                        link(nc.vector.tensor_tensor(lo, lo, s, ALU.mult))
                        link(nc.vector.tensor_tensor(hi, pst[:, 304:320], mean, ALU.subtract))
                        link(nc.vector.tensor_tensor(hi, hi, s, ALU.mult))
                        mn, mx, inv = sc1[:, 0:1], sc1[:, 1:2], sc1[:, 2:3]
                        link(nc.vector.tensor_reduce(mn, lo, X_AXIS, ALU.min))
                        link(nc.vector.tensor_reduce(mx, hi, X_AXIS, ALU.max))
                        link(nc.vector.tensor_tensor(mx, mx, mn, ALU.subtract))
                        link(nc.vector.tensor_scalar(mx, mx, EPS_K, None, ALU.add))
                        link(nc.vector.reciprocal(inv, mx))
                        link(nc.vector.tensor_tensor(t, mean, s, ALU.mult))
                        link(nc.vector.tensor_scalar(t, t, mn, -1.0, ALU.add, ALU.mult))
                        link(nc.vector.tensor_scalar(aff[:, par_, 0, :], s, inv, None, ALU.mult))
                        link(nc.vector.tensor_scalar(aff[:, par_, 1, :], t, inv, None, ALU.mult))

                    def sums(n, k, r):
                        w0, m = SPAN[r]
                        c = n * NG + k
                        if r == 2:
                            dve.wait_ge(s_xn, c + 1)
                            a, b = cols(xn, w0, m), cols(xn, w0 + 1, m)
                        else:
                            src, d = wsum[r // 2][k % 2], STEP[r]
                            dve.wait_ge(s_w[r // 2], c + 1)
                            a, b = cols(src, w0 - d, m), cols(src, w0 + d, m)
                        back = 2 if r < 8 else 1
                        wait(dve, s_ms[r], c + (1 - back))
                        if r > 2:
                            wait(dve, s_pr[r], c + (1 - back))
                        if r == 8:
                            wait(dve, s_w[16], c)
                        nc.vector.tensor_tensor(cols(wsum[r][k % 2], w0, m), a, b, ALU.add).then_inc(s_w[r], 1)

                    def pair2(n, k):
                        c = n * NG + k
                        dve.wait_ge(s_w[2], c + 1)
                        wait(dve, s_l[2], c)
                        w = cols(wsum[2][k % 2], 0, NW)
                        nc.vector.tensor_tensor(pair[2][:, :], w[:, 0, :], w[:, 1, :], ALU.add)\
                            .then_inc(s_pr[2], 1)

                    def prepare(n, par_, k):
                        sums(n, k, 2)
                        pair2(n, k)
                        sums(n, k, 4)
                        sums(n, k, 8)

                    def lower(n, k):
                        l2, l4 = logs[2][0][:, :], logs[4][0][:, :]
                        dve.wait_ge(s_l[2], n * NG + (k + 1))
                        dve.wait_ge(s_l[4], n * NG + (k + 1))
                        nc.vector.scalar_tensor_tensor(l2, l2, 3.0, l4, ALU.mult, ALU.add).then_inc(s_t, 1)

                    def exponent(n, par_, k):
                        l8, l16 = logs[8][k % 2][:, :], logs[16][0][:, :]
                        dve.wait_ge(s_lo, n * NG + (k + 1))
                        dve.wait_ge(s_l[16], n * NG + (k + 1))
                        nc.vector.scalar_tensor_tensor(l8, l16, 3.0, l8, ALU.mult, ALU.add).then_inc(s_f, 1)

                    def output(n, par_, k):
                        dve.wait_ge(s_f, n * NG + (k + 1))
                        dve.wait_ge(s_xd, n * NG + (k + 1))
                        for c in range(GC):
                            dst = group(par_, k)[:, :, c]
                            last = nc.vector.scalar_tensor_tensor(
                                dst, as2(logs[8][k % 2][:, :])[:, :, c], kc[:, GC * k + c:GC * k + c + 1],
                                dst, ALU.mult, ALU.add)
                        last.then_inc(s_o, 1)

                    def step(n, par_, k, entering, before, after):
                        if after:
                            sums(after[0], after[2], 2)
                        if before:
                            exponent(*before)
                        if after:
                            pair2(after[0], after[2])
                        if before:
                            output(*before)
                        if entering:
                            add(*entering[0])
                        if after:
                            sums(after[0], after[2], 4)
                        if entering:
                            extrema(*entering[0])
                        lower(n, k)
                        if len(entering) > 1:
                            add(*entering[1])
                        if after:
                            sums(after[0], after[2], 8)
                        if len(entering) > 1:
                            extrema(*entering[1])

                    def finish(n, par_, k):
                        exponent(n, par_, k)
                        output(n, par_, k)

                    walk(dve, enter, prepare, step, stats, finish)

                @block.gpsimd
                def _(pool):
                    pool.wait_ge(s_pv, PARAM_STEPS)

                    def pairs(n, k, r):
                        c = n * NG + k
                        pool.wait_ge(s_w[r], c + 1)
                        wait(pool, s_ms[r], c)
                        w = cols(wsum[r][k % 2], 0, NW)
                        nc.gpsimd.tensor_tensor(pair[r][:, :], w[:, 0, :], w[:, 1, :], ALU.add)\
                            .then_inc(s_pr[r], 1)

                    def sums16(n, k):
                        src, d = wsum[8][k % 2], STEP[16]
                        pool.wait_ge(s_w[8], n * NG + (k + 1))
                        wait(pool, s_ms[16], n * NG + k)
                        nc.gpsimd.tensor_tensor(cols(wsum[16][0], 0, NW), cols(src, -d, NW), cols(src, d, NW),
                                                ALU.add).then_inc(s_w[16], 1)

                    def shift(n, par_, k):
                        pool.wait_ge(s_xn, n * NG + (k + 1))
                        dc = par[:, 1:2, GC * k:GC * (k + 1)].broadcast_to([P, 2 * NW, GC])
                        nc.gpsimd.tensor_tensor(group(par_, k), group(par_, k), dc, ALU.add)\
                            .then_inc(s_xd, 1)

                    def take_lower(n, k):
                        pool.wait_ge(s_t, n * NG + (k + 1))
                        pool.wait_ge(s_l[8], n * NG + (k + 1))
                        l8 = logs[8][k % 2][:, :]
                        nc.gpsimd.tensor_tensor(l8, l8, logs[2][0][:, :], ALU.subtract).then_inc(s_lo, 1)

                    def prepare(n, par_, k):
                        pairs(n, k, 4)
                        pairs(n, k, 8)

                    def step(n, par_, k, entering, before, after):
                        sums16(n, k)
                        pairs(n, k, 16)
                        shift(n, par_, k)
                        if after:
                            pairs(after[0], after[2], 4)
                        take_lower(n, k)
                        if after:
                            pairs(after[0], after[2], 8)

                    walk(pool, lambda *a: None, prepare, step, lambda *a: None)


SLOT_STEPS = 14
MID_STEPS = 10
PARAM_STEPS = 9
STAT_STEPS = 26

_INS = ["x", "L0_conv_w_re", "L0_conv_w_im", "L0_conv_idx0", "L0_conv_idx1", "L1_conv_gamma",
        "L1_conv_beta", "L1_conv_moving_mean", "L1_conv_moving_var"]


def kernel(**inputs):
    import concourse.bacc as _bacc
    from concourse.bass_utils import run_bass_kernel_spmd as _run

    nc = _bacc.Bacc("TRN2", target_bir_lowering=False, num_devices=1)
    arrays, args = {}, []
    for name in _INS:
        a = np.ascontiguousarray(inputs[name])
        arrays[f"in_{name}"] = a
        args.append(nc.dram_tensor(f"in_{name}", a.shape, mybir.dt.from_np(a.dtype), kind="ExternalInput").ap())
    table = constants()
    arrays["in_table"] = table
    args.append(nc.dram_tensor("in_table", table.shape, F32, kind="ExternalInput").ap())
    args.append(nc.dram_tensor("out_0", (NB, NH, NW, NC), F32, kind="ExternalOutput").ap())
    build(nc, *args)
    r = _run(nc, [arrays], core_ids=[0])
    return r.results[0]["out_0"]
```

```python
from contextlib import ExitStack

import numpy as np

import concourse.bass as bass
from concourse import mybir

F32 = mybir.dt.float32
BF16 = mybir.dt.bfloat16
I32 = mybir.dt.int32
ALU = mybir.AluOpType
ACT = mybir.ActivationFunctionType
X_AXIS = mybir.AxisListType.X

P = 128
NB = 16
NH = NW = 256
NC = 32
NG = 16
GC = NC // NG
NM = 415
KMAX = 16
K1 = KMAX + 1
K0 = 2 * KMAX + 1
NSLOT = K0 * K1
PIX = NH * NW
GROUP = PIX * GC
EPS_GN = 1e-5
EPS_K = 1e-7
EPS_BN = 1e-3
SCALES = (2, 4, 8, 16)
LN2 = float(np.log(2.0))

BAND_FOR = {}
for _r in SCALES:
    if _r == 2:
        _list = [(2, 1, "odd"), (2, 1, "even")]
    else:
        _list = [(_r, 1, "pair"), (_r, 0, "even"), (_r, 0, "odd")]
    for _k in _list:
        BAND_FOR[_k] = len(BAND_FOR)
C_BAND = 0
C_IDENT = C_BAND + P * len(BAND_FOR)
C_ONES = C_IDENT + P
C_BH = C_ONES + P
C_FI = C_BH + 2 * P
C_KEEP = C_FI + NW
C_BF = C_KEEP
C_FB = C_BF + 2 * K0
C_CEN = C_FB + 4 * 4 * K1
C_PAIR = C_CEN + 64
C_GRP = C_PAIR + 64
C_END = C_GRP + 64


def constants():
    t = np.zeros((P, C_END), np.float64)
    p = np.arange(P)
    for (r, e, src), i in BAND_FOR.items():
        out_row = 2 * p[None, :] + e
        lo, hi = out_row - (r // 2 - 1), out_row + r // 2
        if src == "pair":
            band = (2 * p[:, None] >= lo) & (2 * p[:, None] + 1 <= hi)
        else:
            row = 2 * p[:, None] + (src == "odd")
            band = (row >= lo) & (row <= hi)
        t[:, C_BAND + i * P:C_BAND + (i + 1) * P] = band
    t[:, C_IDENT:C_IDENT + P] = np.eye(P)
    t[:, C_ONES:C_ONES + P] = 1.0
    turn = 2 * np.pi / NH
    k1 = np.arange(K1)
    for q in range(2):
        h = 2 * p + q
        for a in range(1, KMAX + 1):
            t[a, C_BH + q * P:C_BH + (q + 1) * P] = np.sin(turn * (a * h % NH))
            t[K1 + a - 1, C_BH + q * P:C_BH + (q + 1) * P] = np.cos(turn * (a * h % NH))
            t[:, C_BF + q * K0 + 2 * a - 1] = np.cos(turn * (a * h % NH))
            t[:, C_BF + q * K0 + 2 * a] = np.sin(turn * (a * h % NH))
        t[0, C_BH + q * P:C_BH + (q + 1) * P] = 1.0
        t[:, C_BF + q * K0] = 1.0
    weight = np.where(k1 == 0, 1.0, 2.0) / PIX
    ang = turn * (k1[:, None] * np.arange(NW)[None, :] % NW)
    t[0:K1, C_FI:C_FI + NW] = weight[:, None] * np.cos(ang)
    t[32:32 + K1, C_FI:C_FI + NW] = weight[:, None] * np.sin(ang)
    for v in range(2):
        ang = turn * ((P * v + p)[:, None] * k1[None, :] % NW)
        c, s = np.cos(ang), np.sin(ang)
        at = C_FB + v * 8 * K1
        t[:, at:at + 4 * K1] = np.concatenate([c, -s, c, -s], 1)
        t[:, at + 4 * K1:at + 8 * K1] = np.concatenate([-s, -c, s, c], 1)
    e = np.eye(32)
    pair = np.kron(np.eye(NG), np.full((GC, GC), 1.0 / GC))
    t[0:32, C_CEN:C_CEN + 32] = e - pair
    t[32:64, C_CEN + 32:C_CEN + 64] = e
    t[0:32, C_PAIR:C_PAIR + 32] = pair / PIX
    t[0:32, C_PAIR + 32:C_PAIR + 64] = pair / PIX
    spread = np.kron(np.eye(NG), np.ones((1, GC))) / GROUP
    t[0:NG, C_GRP:C_GRP + 32] = spread
    t[0:NG, C_GRP + 32:C_GRP + 64] = spread
    return t.astype(np.float32)


ENTER = {k: [] for k in range(NG)}
for _g in range(NG):
    ENTER[6 + _g // 2].append(_g)
STATS_AT = 14

LO, HI = 7, 8
WP = NW + LO + HI
SPAN = {2: (-7, 270), 4: (-6, 268), 8: (-4, 264), 16: (0, 256)}
STEP = {4: 1, 8: 2, 16: 4}


def build(nc, x, w_re, w_im, idx0, idx1, gamma, beta, mov_mean, mov_var, table, out):
    ctx = ExitStack()
    with ctx:
        def sb(name, shape, dt=F32):
            return ctx.enter_context(nc.sbuf_tensor(name, shape, dt))

        def sem(name):
            return ctx.enter_context(nc.semaphore(name))

        wtab = nc.dram_tensor("wtab", [NSLOT + 1, 64, 64], F32, kind="Internal").ap()
        vtab = [nc.dram_tensor("vtab_even", [2, K1 * K1, NB, NC], F32, kind="Internal").ap(),
                nc.dram_tensor("vtab_odd", [2, KMAX * K1, NB, NC], F32, kind="Internal").ap()]

        arena = sb("arena", [P, 2 * 2 * NW * NC])
        cst = sb("cst", [P, C_KEEP])
        ssqb = sb("ssqb", [NG, NB])
        half = NW * NC
        xbuf = [arena[:, n * 2 * half:(n + 1) * 2 * half] for n in range(2)]

        early = ExitStack()
        cst1 = early.enter_context(nc.sbuf_tensor("cst1", [P, C_END - C_KEEP], F32))

        def const(at, rows, cols):
            if at >= C_KEEP:
                return cst1[0:rows, at - C_KEEP:at - C_KEEP + cols]
            return cst[0:rows, at:at + cols]

        def wait(eng, semaphore, count):
            if not isinstance(count, int) or count > 0:
                eng.wait_ge(semaphore, count)

        ident = const(C_IDENT, P, P)
        ones = const(C_ONES, P, P)

        with ExitStack() as one:
            def psum1(name, shape):
                return one.enter_context(nc.psum_tensor(name, shape, F32))

            psr = psum1("psr", [P, 2, 512])
            psz = psum1("psz", [P, 2, 512])
            psx = psum1("psx", [P, 3, 512])
            pss = psum1("pss", [P, 512])
            xh = [arena[:, v * half:(v + 1) * half].rearrange("p (q w c) -> p q w c", q=2, w=P)
                  for v in range(2)]
            at = 2 * half
            modes_all = arena[:, at:at + NSLOT * NB].rearrange("p (s b) -> p s b", b=NB)
            modes = modes_all[0:64]
            at += NSLOT * NB
            zsb = arena[:, at:at + 2 * K0 * NC].rearrange("p (v k c) -> p v k c", v=2, k=K0)
            at += 2 * K0 * NC
            wrow = arena[0:83, 4 * half - 4096:4 * half].rearrange("p (i o) -> p i o", i=64)
            assert at <= 4 * half - 4096
            rsb = [one.enter_context(nc.sbuf_tensor(f"rsb{v}", [P, P * NC], F32)) for v in range(2)]
            NJ = 4
            junk1 = one.enter_context(nc.sbuf_tensor("junk1", [P, 2, NJ, 512], BF16))
            ssq1 = one.enter_context(nc.sbuf_tensor("ssq1", [P, 2, NG], F32))
            zero = one.enter_context(nc.sbuf_tensor("zero", [P, 1024], F32))
            wraw = one.enter_context(nc.sbuf_tensor("wraw", [83, 2, NC * NC], F32))
            idx = one.enter_context(nc.sbuf_tensor("idx", [83, 2, 5], I32))
            sl = one.enter_context(nc.sbuf_tensor("sl", [83, 6, 5], F32))
            slot = one.enter_context(nc.sbuf_tensor("slot", [83, 5], I32))

            s_cst = sem("consts_in")
            s_xin = [sem(f"x_half_in{v}") for v in range(2)]
            s_xsq = [sem(f"x_half_squared{v}") for v in range(2)]
            s_r = [sem(f"rows_done{v}") for v in range(2)]
            s_re = [sem(f"rows_kept{v}") for v in range(2)]
            s_rz = sem("row_zeros_set")
            s_z = [sem(f"columns_turned{v}") for v in range(2)]
            s_ze = [sem(f"columns_kept{v}") for v in range(2)]
            s_m = [sem(f"modes_done{k}") for k in range(3)]
            s_me = [sem(f"modes_kept{k}") for k in range(3)]
            s_ss = sem("squares_summed")
            s_sse = sem("squares_kept")
            s_idx = sem("indices_in")
            s_sl = sem("slot_steps")
            s_zero = sem("zero_set")
            s_clear = sem("table_cleared")
            s_wrow = sem("weight_rows_built")
            s_wraw = sem("weights_raw_in")
            s_scat = sem("weight_rows_out")
            s_mzero = sem("mode_zeros_set")

            NR = P * NC // 512
            NT = NC // 8
            XA = [(0, 15), (15, 14), (29, 4)]
            xv = x.rearrange("b (p q) (v w) c -> b v p q (w c)", q=2, v=2)

            with nc.Block() as block:
                @block.sync
                def _(sync):
                    sync.dma_start(cst[:, :], table[:, 0:C_KEEP]).then_inc(s_cst, 16)
                    sync.dma_start(cst1[:, :], table[:, C_KEEP:C_END]).then_inc(s_cst, 16)

                    def load(n):
                        for v in range(2):
                            wait(sync, s_xsq[v], n * NG)
                            wait(sync, s_r[v], n * 2 * NR)
                            sync.dma_start(xh[v].rearrange("p q w c -> p q (w c)"),
                                           xv[bass.ds(n, 1), v].rearrange("b p q m -> (b p) q m"))\
                                .then_inc(s_xin[v], 16)

                    load(0)
                    with sync.Fori(1, NB) as n:
                        load(n)

                @block.gpsimd
                def _(pool):
                    pool.memset(zero[:, :], 0.0).then_inc(s_zero, 1)
                    pool.dma_start(idx[:, 0, :], idx0.rearrange("(p t) -> p t", p=83)).then_inc(s_idx, 16)
                    pool.dma_start(idx[:, 1, :], idx1.rearrange("(p t) -> p t", p=83)).then_inc(s_idx, 16)
                    pool.wait_ge(s_zero, 1)
                    flat = wtab.rearrange("s i o -> s (i o)")
                    done = 0
                    while done < NSLOT + 1:
                        k = min(P, NSLOT + 1 - done)
                        pool.dma_start(flat[done:done + k, :].rearrange("s (r m) -> s r m", r=4),
                                       zero[0:k, :].rearrange("p (r m) -> p r m", r=1).broadcast_to([k, 4, 1024]))\
                            .then_inc(s_clear, 16)
                        done += k
                    pool.wait_ge(s_clear, 16 * 5)
                    pool.wait_ge(s_sl, SLOT_STEPS)
                    for t in range(5):
                        for j, w in enumerate((w_re, w_im)):
                            pool.dma_start(wraw[:, j], w.rearrange("(p t) i o -> t p (i o)", p=83)[t])\
                                .then_inc(s_wraw, 16)
                        if t:
                            pool.wait_ge(s_scat, 16 * t)
                        pool.wait_ge(s_wraw, 32 * (t + 1))
                        re, im = (wraw[:, j, :].rearrange("p (i o) -> p i o", i=NC) for j in range(2))
                        pool.tensor_copy(wrow[:, 0:32, 0:32], re).then_inc(s_wrow, 1)
                        pool.tensor_copy(wrow[:, 0:32, 32:64], im).then_inc(s_wrow, 1)
                        pool.tensor_copy(wrow[:, 32:64, 32:64], re).then_inc(s_wrow, 1)
                        pool.tensor_scalar(wrow[:, 32:64, 0:32], im, -1.0, None, ALU.mult).then_inc(s_wrow, 1)
                        pool.wait_ge(s_wrow, 4 * (t + 1))
                        pool.indirect_dma_start(
                            flat, bass.IndirectOffsetOnAxis(ap=slot[:, t:t + 1], axis=0),
                            wrow.rearrange("p i o -> p (i o)"), None).then_inc(s_scat, 16)
                    pool.wait_ge(s_scat, 16 * 5)

                @block.scalar
                def _(act):
                    def squares(n):
                        for v in range(2):
                            act.wait_ge(s_xin[v], n * 16 + 16)
                            if v == 0:
                                wait(act, s_ss, n)
                            for g in range(NG):
                                wait(act, s_xsq[v], n * NG + max(g - NJ + 1, 0))
                                nc.scalar.activation(
                                    junk1[:, v, g % NJ, :].rearrange("p (w c) -> p w c", c=GC),
                                    xh[v].rearrange("p q w c -> p (q w) c")[:, :, GC * g:GC * (g + 1)],
                                    ACT.Square, accum_out=ssq1[:, v, g:g + 1]).then_inc(s_xsq[v], 1)

                    squares(0)
                    with act.Fori(1, NB) as n:
                        squares(n)

                @block.vector
                def _(dve):
                    nc.vector.memset(modes_all[64:128], 0.0).then_inc(s_mzero, 1)
                    steps = [0]

                    def link(ins):
                        steps[0] += 1
                        ins.then_inc(s_sl, 1)
                        dve.wait_ge(s_sl, steps[0])

                    dve.wait_ge(s_idx, 32)
                    k0, k1, hi, t0, t1, t2 = (sl[:, j, :] for j in range(6))
                    link(nc.vector.tensor_copy(k0, idx[:, 0, :]))
                    link(nc.vector.tensor_copy(k1, idx[:, 1, :]))
                    link(nc.vector.tensor_scalar(hi, k0, float(NH // 2), -float(NH), ALU.is_ge, ALU.mult))
                    link(nc.vector.tensor_tensor(k0, k0, hi, ALU.add))
                    link(nc.vector.tensor_scalar(hi, k0, 0.0, None, ALU.is_gt))
                    link(nc.vector.tensor_scalar(t0, k0, -1.0, None, ALU.mult))
                    link(nc.vector.tensor_tensor(t0, k0, t0, ALU.max))
                    link(nc.vector.tensor_tensor(t1, t0, k1, ALU.max))
                    link(nc.vector.tensor_scalar(t1, t1, float(KMAX), float(2 * NSLOT), ALU.is_gt, ALU.mult))
                    link(nc.vector.scalar_tensor_tensor(t2, hi, float(KMAX), t0, ALU.mult, ALU.add))
                    link(nc.vector.scalar_tensor_tensor(t2, t2, float(K1), k1, ALU.mult, ALU.add))
                    link(nc.vector.tensor_tensor(t2, t2, t1, ALU.add))
                    link(nc.vector.tensor_scalar(t2, t2, float(NSLOT), None, ALU.min))
                    link(nc.vector.tensor_copy(slot[:, :], t2))
                    assert steps[0] == SLOT_STEPS

                    def keep(n):
                        for v in range(2):
                            for i in range(NR):
                                dve.wait_ge(s_r[v], n * 2 * NR + 2 * (i + 1))
                                if i == 0:
                                    wait(dve, s_z[v], n * NT)
                                nc.vector.tensor_copy(rsb[v][0:K0, i * 512:(i + 1) * 512], psr[0:K0, i % 2, :])\
                                    .then_inc(s_re[v], 1)
                            if v == 0 and not (isinstance(n, int) and n == 0):
                                keep_modes(n - 1)
                            for i in range(NT):
                                dve.wait_ge(s_z[v], n * NT + (i + 1))
                                nc.vector.tensor_copy(
                                    zsb[:, v, :, i * 8:(i + 1) * 8].rearrange("p k c -> p c k"),
                                    psz[:, i % 2, 0:8 * K0].rearrange("p (c k) -> p c k", c=8))\
                                    .then_inc(s_ze[v], 1)

                    def keep_modes(n):
                        for k, (j0, m) in enumerate(XA):
                            dve.wait_ge(s_m[k], n + 1)
                            for ri in range(2):
                                out_rows = modes[32 * ri:32 * ri + 32]
                                bank = psx[0:32, k, 0:m * 2 * K1].rearrange("p (j r f) -> p j r f", j=m, r=2)
                                if k == 0:
                                    nc.vector.tensor_copy(
                                        out_rows[:, 0:K1, bass.ds(n, 1)].rearrange("p f b -> p (f b)"),
                                        bank[:, 0, ri, :])
                                a0, na, skip = (j0 + 1 if k else 2) // 2, m // 2, m % 2
                                for sign in range(2):
                                    s0 = (a0 + KMAX * (1 - sign)) * K1
                                    last = nc.vector.tensor_copy(
                                        out_rows[:, s0:s0 + na * K1, bass.ds(n, 1)]
                                        .rearrange("p (a f) b -> p a (f b)", a=na),
                                        bank[:, skip + sign::2, ri, :])
                            last.then_inc(s_me[k], 1)
                        dve.wait_ge(s_ss, n + 1)
                        nc.vector.tensor_copy(ssqb[:, bass.ds(n, 1)], pss[0:NG, 0:1]).then_inc(s_sse, 1)

                    nc.vector.memset(rsb[0][:, :], 0.0).then_inc(s_rz, 1)
                    nc.vector.memset(rsb[1][:, :], 0.0).then_inc(s_rz, 1)
                    dve.wait_ge(s_rz, 2)
                    keep(0)
                    with dve.Fori(1, NB) as n:
                        keep(n)
                    keep_modes(NB - 1)

                @block.tensor
                def _(pe):
                    pe.wait_ge(s_cst, 32)
                    def over_rows(n, v):
                        pe.wait_ge(s_xin[v], n * 16 + 16)
                        flat = xh[v].rearrange("p q w c -> p q (w c)")
                        for i in range(NR):
                            if i >= 2:
                                pe.wait_ge(s_re[v], n * NR + (i - 1))
                            elif v == 1:
                                pe.wait_ge(s_re[0], n * NR + (NR - 1 + i))
                            else:
                                wait(pe, s_re[1], n * NR + (i - 1) if not isinstance(n, int) or n else 0)
                            for q in range(2):
                                nc.tensor.matmul(psr[0:K0, i % 2, :], const(C_BF + q * K0, P, K0),
                                                 flat[:, q, i * 512:(i + 1) * 512],
                                                 start=(q == 0), stop=(q == 1)).then_inc(s_r[v], 1)

                    def turn(n, v):
                        pe.wait_ge(s_re[v], n * NR + NR)
                        w_last = rsb[v][:, :].rearrange("p (w c) -> p w c", c=NC)
                        for i in range(NT):
                            if i >= 2:
                                pe.wait_ge(s_ze[v], n * NT + (i - 1))
                            elif v == 1:
                                pe.wait_ge(s_ze[0], n * NT + (NT - 1 + i))
                            else:
                                wait(pe, s_ze[1], n * NT + (i - 1) if not isinstance(n, int) or n else 0)
                            nc.tensor.transpose(psz[:, i % 2, 7 * K0:7 * K0 + P],
                                                w_last[:, :, i * 8 + 7], ident)
                            for c in range(7):
                                last = nc.tensor.transpose(psz[:, i % 2, c * K0:(c + 1) * K0],
                                                           w_last[0:K0, :, i * 8 + c], ident[0:K0, 0:K0])
                            last.then_inc(s_z[v], 1)

                    def transform(n):
                        if not (isinstance(n, int) and n == 0):
                            over_squares(n - 1)
                        for v in range(2):
                            over_rows(n, v)
                            if v == 0 and not (isinstance(n, int) and n == 0):
                                over_columns(n - 1)
                            turn(n, v)

                    def over_columns(n):
                        pe.wait_ge(s_ze[0], n * NT + NT)
                        pe.wait_ge(s_ze[1], n * NT + NT)
                        for k, (j0, m) in enumerate(XA):
                            wait(pe, s_me[k], n)
                            j = j0
                            while j < j0 + m:
                                cols = (4 if j else 2) * K1
                                comps = [(0, 0)] if j == 0 else [(j, 0), (j + 1, 1)]
                                ops = [(v, comp, kind) for comp, kind in comps for v in range(2)]
                                for i, (v, comp, kind) in enumerate(ops):
                                    last = nc.tensor.matmul(
                                        psx[0:32, k, (j - j0) * 2 * K1:(j - j0) * 2 * K1 + cols],
                                        zsb[:, v, comp, :],
                                        const(C_FB + v * 8 * K1 + kind * 4 * K1, P, cols),
                                        start=(i == 0), stop=(i == len(ops) - 1))
                                j += 2 if j else 1
                            last.then_inc(s_m[k], 1)

                    def over_squares(n):
                        for v in range(2):
                            pe.wait_ge(s_xsq[v], n * NG + NG)
                        wait(pe, s_sse, n)
                        for v in range(2):
                            last = nc.tensor.matmul(pss[0:NG, 0:1], ssq1[:, v, :], ones[:, 0:1],
                                                    start=(v == 0), stop=(v == 1))
                        last.then_inc(s_ss, 1)

                    transform(0)
                    with pe.Fori(1, NB) as n:
                        transform(n)
                    over_squares(NB - 1)
                    over_columns(NB - 1)

        with ExitStack() as mid:
            def psum2(name, shape):
                return mid.enter_context(nc.psum_tensor(name, shape, F32))

            psy = psum2("psymix", [P, 4, 512])
            psq = psum2("psq", [P, 4, 512])
            NWT = 3
            wt_all = mid.enter_context(nc.sbuf_tensor("wt", [P, NWT, K1, 64], F32))
            wt = [wt_all[:, j] for j in range(NWT)]
            BLOCKS = [(0, 0, 7), (0, 7, 7), (0, 14, 3), (1, 0, 7), (1, 7, 7), (1, 14, 2)]
            turned = mid.enter_context(nc.sbuf_tensor("turned", [P, len(BLOCKS), NB, 64], F32))
            st = mid.enter_context(nc.sbuf_tensor("st", [64, 6, NB], F32))

            s_st = sem("stat_matmuls")
            s_stv = sem("stat_steps")
            s_sta = sem("stat_logs")
            s_wt = [sem(f"weights_in{j}") for j in range(NWT)]
            s_mix = [sem(f"mixed{j}") for j in range(NWT)]
            s_mixe = [sem(f"mixed_kept{j}") for j in range(NWT)]
            s_yc = sem("modes_combined")
            s_v = [sem(f"turned{j}") for j in range(4)]
            s_vd = [sem(f"turned_kept_dve{j}") for j in range(4)]
            s_va = [sem(f"turned_kept_act{j}") for j in range(4)]
            s_vdone = sem("blocks_kept")
            s_vout = sem("parts_out")
            s_vz = sem("weight_zeros_set")
            s_x0 = sem("x_first_in")

            with nc.Block() as block:
                @block.sync
                def _(sync):
                    def load(buf, turn_no, j):
                        wait(sync, s_mix[buf], turn_no)
                        sync.dma_start(wt[buf][0:64], wtab[bass.ds(j * K1, K1)].rearrange("s i o -> i s o"))\
                            .then_inc(s_wt[buf], 16)

                    for buf, j in enumerate((0, K1, 1)):
                        load(buf, 0, j)
                    sync.dma_start(xbuf[0], x.rearrange("b (p q) w c -> b p (q w c)", q=2)[0]).then_inc(s_x0, 16)
                    with sync.Fori(1, KMAX) as a:
                        load(1, a, a + K1)
                        load(2, a, a + 1)
                    for i, (odd, j0, m) in enumerate(BLOCKS):
                        for j in range(2):
                            bank = (2 * i + j) % 4
                            turn_no = (2 * i + j) // 4 + 1
                            sync.wait_ge(s_vd[bank], turn_no)
                            sync.wait_ge(s_va[bank], turn_no)
                        r0 = j0 * K1
                        for part in range(2):
                            sync.dma_start(vtab[odd][part, r0:r0 + m * K1],
                                           turned[0:m * K1, i, :, part * NC:(part + 1) * NC])\
                                .then_inc(s_vout, 16)
                    sync.wait_ge(s_vout, 16 * 2 * len(BLOCKS))
                    sync.wait_ge(s_x0, 16)

                @block.scalar
                def _(act):
                    act.wait_ge(s_stv, 4)
                    nc.scalar.activation(st[:, 2, :], st[:, 1, :], ACT.Ln).then_inc(s_sta, 1)
                    act.wait_ge(s_sta, 1)
                    nc.scalar.activation(st[:, 2, :], st[:, 2, :], ACT.Exp, scale=-0.5).then_inc(s_sta, 1)
                    for i, (odd, j0, m) in enumerate(BLOCKS):
                        for j in range(2):
                            bank, turn_no = (2 * i + j) % 4, (2 * i + j) // 4 + 1
                            act.wait_ge(s_vd[bank], turn_no)
                            src = psq[0:m * K1, bank, :].rearrange("p (b o) -> p b o", b=8)
                            nc.scalar.activation(turned[0:m * K1, i, 8 * j:8 * j + 8, NC:2 * NC],
                                                 src[:, :, NC * odd:NC * odd + NC], ACT.Copy,
                                                 scale=-1.0 if odd else 1.0).then_inc(s_va[bank], 1)

                @block.vector
                def _(dve):
                    steps = [0]

                    def link(ins):
                        steps[0] += 1
                        ins.then_inc(s_stv, 1)
                        dve.wait_ge(s_stv, steps[0])

                    nc.vector.memset(wt_all[64:128], 0.0).then_inc(s_vz, 1)
                    dve.wait_ge(s_st, 1)
                    link(nc.vector.tensor_copy(st[:, 0, :], psy[0:64, 0, 0:NB]))
                    link(nc.vector.tensor_tensor(st[:, 0, :], st[:, 0, :], st[:, 0, :], ALU.mult))
                    link(nc.vector.tensor_tensor(st[:, 1, :], psy[0:64, 1, 0:NB], st[:, 0, :], ALU.subtract))
                    link(nc.vector.tensor_scalar(st[:, 1, :], st[:, 1, :], 0.0, EPS_GN, ALU.max, ALU.add))
                    dve.wait_ge(s_sta, 2)
                    link(nc.vector.tensor_tensor(st[:, 3, :], st[:, 2, :], st[:, 2, :], ALU.mult))
                    link(nc.vector.tensor_tensor(st[:, 3, :], st[:, 3, :], st[:, 1, :], ALU.mult))
                    link(nc.vector.tensor_scalar(st[:, 3, :], st[:, 3, :], -0.5, 1.5, ALU.mult, ALU.add))
                    link(nc.vector.tensor_tensor(st[:, 4, :], st[:, 3, :], st[:, 2, :], ALU.mult))
                    link(nc.vector.tensor_copy(modes[:, 0, :], psy[0:64, 2, 0:NB]))
                    link(nc.vector.tensor_tensor(
                        modes, modes, st[:, 4:5, :].broadcast_to([64, NSLOT, NB]), ALU.mult))

                    def slots(j, k):
                        return modes[:, bass.ds(j * K1, k * K1), :].rearrange("p s b -> p (s b)")

                    def mixed(j):
                        return psy[0:64, j, 0:K1 * NB]

                    dve.wait_ge(s_mix[0], 1)
                    zero_row = modes[:, 0:K1, :].rearrange("p s b -> p (s b)")
                    nc.vector.tensor_scalar(zero_row[0:32], mixed(0)[32:64], -1.0, None, ALU.mult)
                    nc.vector.tensor_copy(zero_row[32:64], mixed(0)[0:32]).then_inc(s_mixe[0], 1)
                    with dve.Fori(0, KMAX) as a:
                        dve.wait_ge(s_mix[1], a + 1)
                        nc.vector.tensor_copy(slots(a + K1, 1), mixed(1)).then_inc(s_mixe[1], 1)
                        dve.wait_ge(s_mix[2], a + 1)
                        dve.wait_ge(s_mixe[1], a + 1)
                        nc.vector.tensor_tensor(slots(a + 1, 1), mixed(2), slots(a + K1, 1), ALU.subtract)
                        nc.vector.tensor_tensor(slots(a + K1, 1), mixed(2), slots(a + K1, 1), ALU.add)\
                            .then_inc(s_mixe[2], 1)
                    for i, (odd, j0, m) in enumerate(BLOCKS):
                        for j in range(2):
                            bank, turn_no = (2 * i + j) % 4, (2 * i + j) // 4 + 1
                            dve.wait_ge(s_v[bank], turn_no)
                            src = psq[0:m * K1, bank, :].rearrange("p (b o) -> p b o", b=8)
                            nc.vector.tensor_copy(turned[0:m * K1, i, 8 * j:8 * j + 8, 0:NC],
                                                  src[:, :, NC * (1 - odd):NC * (1 - odd) + NC])\
                                .then_inc(s_vd[bank], 1)

                @block.tensor
                def _(pe):
                    nc.tensor.matmul(psy[0:64, 0, 0:NB], const(C_PAIR, 64, 64), modes[:, 0, :],
                                     start=True, stop=True)
                    nc.tensor.matmul(psy[0:64, 1, 0:NB], const(C_GRP, NG, 64), ssqb[:, :],
                                     start=True, stop=True)
                    nc.tensor.matmul(psy[0:64, 2, 0:NB], const(C_CEN, 64, 64), modes[:, 0, :],
                                     start=True, stop=True).then_inc(s_st, 1)
                    pe.wait_ge(s_stv, MID_STEPS)
                    pe.wait_ge(s_vz, 1)

                    def mix(buf, turn_no, j):
                        pe.wait_ge(s_wt[buf], turn_no * 16 + 16)
                        wait(pe, s_mixe[buf], turn_no)
                        for s in range(K1):
                            last = nc.tensor.matmul(
                                psy[0:64, buf, s * NB:(s + 1) * NB], wt[buf][:, s, :],
                                modes_all[:, bass.ds(j * K1 + s, 1), :].rearrange("p s b -> p (s b)"),
                                start=True, stop=True)
                        last.then_inc(s_mix[buf], 1)

                    mix(0, 0, 0)
                    mix(1, 0, K1)
                    mix(2, 0, 1)
                    with pe.Fori(1, KMAX) as a:
                        mix(1, a, a + K1)
                        mix(2, a, a + 1)
                    pe.wait_ge(s_mixe[0], 1)
                    pe.wait_ge(s_mixe[2], KMAX)
                    for i, (odd, j0, m) in enumerate(BLOCKS):
                        for j in range(2):
                            bank, turn_no = (2 * i + j) % 4, (2 * i + j) // 4 + 1
                            wait(pe, s_va[bank], turn_no - 1)
                            for b in range(8):
                                last = nc.tensor.transpose(
                                    psq[0:m * K1, bank, b * 64:(b + 1) * 64],
                                    modes[:, (odd * K1 + j0) * K1:(odd * K1 + j0 + m) * K1, 8 * j + b],
                                    ident[0:64, 0:64])
                            last.then_inc(s_v[bank], 1)

        early.close()
        with ExitStack() as two:
            def sb2(name, shape, dt=F32):
                return two.enter_context(nc.sbuf_tensor(name, shape, dt))

            def psum3(name, shape):
                return two.enter_context(nc.psum_tensor(name, shape, F32))

            NPX = NW * GC
            vin = sb2("vin", [P, K0, NC])
            usb = [sb2(f"usb{i}", [K0, NPX]) for i in range(2)]
            xn = sb2("xn", [P, 2, WP * GC])
            wsum = {2: [sb2(f"w2_{i}", [P, 2, WP * GC]) for i in range(2)],
                    4: [sb2(f"w4_{i}", [P, 2, WP * GC]) for i in range(2)]}
            wsum[8] = [sb2("w8", [P, 2, WP * GC])] * 2
            wsum[16] = [sb2("w16", [P, 2, NPX])] * 2
            pair = {r: sb2(f"pair{r}", [P, NPX]) for r in SCALES}
            logs = {2: [sb2("log2", [P, 2 * NPX])] * 2,
                    4: [sb2("log4", [P, 2 * NPX])] * 2,
                    8: [sb2(f"log8_{i}", [P, 2 * NPX]) for i in range(2)],
                    16: [sb2("log16", [P, 2 * NPX])] * 2}
            junk = sb2("junk", [P, 2 * NPX], BF16)
            stat = sb2("stat", [P, 4 * NG])
            red = sb2("red", [32, 2])
            diag = sb2("diag", [32, 64])
            sm = sb2("sm", [P, 8, NG])
            sc1 = sb2("sc1", [P, 4])
            aff = sb2("aff", [P, 2, 2, NG])
            par = sb2("par", [P, 2, NC])
            raw = sm[:, :, :].rearrange("p a g -> p (a g)").rearrange("p (j c) -> p j c", c=NC)
            eps_k = sb2("eps_k", [P, 1])[:, :]

            psu = psum3("psu", [P, 512])
            psy = psum3("psy", [P, 2, 512])
            psm = [psum3(f"psm{i}", [P, 2, 512]) for i in range(2)]
            pst = psum3("pst", [P, 512])

            s_par = sem("params_in")
            s_pv = sem("param_steps")
            s_pa = sem("param_logs")
            s_x = [sem(f"x_in{i}") for i in range(2)]
            s_out = [sem(f"out_stored{i}") for i in range(2)]
            s_vin = sem("parts_in")
            s_u = sem("columns_done")
            s_us = sem("columns_kept")
            s_y = sem("y_done")
            s_x1 = sem("x1_done")
            s_mm = sem("min_max_done")
            s_sq = sem("x1_squared")
            s_t1 = sem("stat_sums_done")
            s_t2 = sem("extrema_spread")
            s_tv = sem("stat2_steps")
            s_ta = sem("stat2_logs")
            s_xn = sem("scaled_ready")
            s_pad = sem("pads_zeroed")
            s_w = {r: sem(f"row_sums{r}_ready") for r in SCALES}
            s_pr = {r: sem(f"pair{r}_ready") for r in SCALES}
            s_ms = {r: sem(f"measure{r}_done") for r in SCALES}
            s_l = {r: sem(f"log{r}_ready") for r in SCALES}
            s_t = sem("log4_plus_3_log2_ready")
            s_lo = sem("lower_logs_taken_off_log8")
            s_f = sem("exponent_ready")
            s_xd = sem("x1_shifted")
            s_o = sem("outputs_done")

            xs = x.rearrange("b (p q) w c -> b p (q w c)", q=2)
            os_ = out.rearrange("b (p q) w c -> b p (q w c)", q=2)

            def group(par_, g):
                return xbuf[par_].rearrange("p (m c) -> p m c", c=NC)[:, :, GC * g:GC * (g + 1)]

            def as2(ap):
                return ap.rearrange("p (m c) -> p m c", c=GC)

            def cols(ap, w0, m):
                if ap.shape[-1] == NPX:
                    return ap[:, :, w0 * GC:(w0 + m) * GC]
                return ap[:, :, (w0 + LO) * GC:(w0 + LO + m) * GC]

            def walk(eng, enter, prepare, step, stats, finish=None):
                def sample(n, par_):
                    last = isinstance(n, int) and n == NB - 1
                    for k in range(NG):
                        entering = [] if last else [(n + 1, 1 - par_, g) for g in ENTER[k]]
                        after = (n, par_, k + 1) if k + 1 < NG else None if last else (n + 1, 1 - par_, 0)
                        before = (n, par_, k - 1) if k else None if isinstance(n, int) and n == 0 else \
                            (n - 1, 1 - par_, NG - 1)
                        step(n, par_, k, entering, before, after)
                        if not last and k == STATS_AT:
                            stats(n + 1, 1 - par_)

                for g in range(NG):
                    enter(0, 0, g)
                stats(0, 0)
                prepare(0, 0, 0)
                sample(0, 0)
                with eng.Fori(0, NB // 2 - 1) as two_samples:
                    sample(two_samples * 2 + 1, 1)
                    sample(two_samples * 2 + 2, 0)
                sample(NB - 1, 1)
                if finish:
                    finish(NB - 1, 1, NG - 1)

            with nc.Block() as block:
                @block.sync
                def _(sync):
                    for j, p_ in enumerate((gamma, beta, mov_mean, mov_var)):
                        sync.dma_start(raw[:, j, :], p_.rearrange("(a c) -> a c", a=1).broadcast_to([P, NC]))\
                            .then_inc(s_par, 16)

                    def load(n, par_):
                        sync.dma_start(xbuf[par_], xs[bass.ds(n, 1)].rearrange("b p m -> (b p) m"))\
                            .then_inc(s_x[par_], 16)

                    def load_parts(n):
                        wait(sync, s_u, n * NG)
                        for odd, (k0, m) in enumerate(((0, K1), (K1, KMAX))):
                            for part in range(2):
                                sync.dma_start(
                                    vin[32 * part:32 * part + K1, k0:k0 + m, :],
                                    vtab[odd].rearrange("t (a f) b c -> b t f a c", f=K1)
                                    [bass.ds(n, 1), part].rearrange("b f a c -> (b f) a c"))\
                                    .then_inc(s_vin, 16)

                    def store(n, par_):
                        sync.wait_ge(s_o, n * NG + NG)
                        sync.dma_start(os_[bass.ds(n, 1)].rearrange("b p m -> (b p) m"), xbuf[par_])\
                            .then_inc(s_out[par_], 16)

                    def turn(n, par_):
                        load_parts(n + 2)
                        store(n, par_)
                        sync.wait_ge(s_out[par_], n * 8 + (16 - 8 * par_))
                        load(n + 2, par_)

                    sync.wait_ge(s_pad, 3)
                    load_parts(0)
                    load(1, 1)
                    load_parts(1)
                    turn(0, 0)
                    with sync.Fori(0, NB // 2 - 2) as two_samples:
                        turn(two_samples * 2 + 1, 1)
                        turn(two_samples * 2 + 2, 0)
                    turn(NB - 3, 1)
                    store(NB - 2, 0)
                    store(NB - 1, 1)
                    for par_ in range(2):
                        sync.wait_ge(s_out[par_], 16 * NB // 2)

                @block.tensor
                def _(pe):
                    pe.wait_ge(s_pad, 3)

                    def columns(n, par_, g):
                        if g == 0:
                            pe.wait_ge(s_vin, n * 64 + 64)
                        wait(pe, s_us, n * NG + g)
                        for c in range(GC):
                            last = nc.tensor.matmul(psu[0:K0, c * NW:(c + 1) * NW],
                                                    vin[:, :, GC * g + c],
                                                    const(C_FI, P, NW), start=True, stop=True)
                        last.then_inc(s_u, 1)

                    def rows(n, par_, g):
                        pe.wait_ge(s_us, n * NG + (g + 1))
                        wait(pe, s_x1, n * NG + g)
                        for q in range(2):
                            last = nc.tensor.matmul(psy[:, q, :], const(C_BH + q * P, K0, P), usb[g % 2][:, :],
                                                    start=True, stop=True)
                        last.then_inc(s_y, 1)

                    def enter(n, par_, g):
                        columns(n, par_, g)
                        rows(n, par_, g)

                    def spread(n):
                        pe.wait_ge(s_tv, n * STAT_STEPS + 6)
                        nc.tensor.matmul(pst[:, 256:320], ones[0:32, :], diag[:, :],
                                         start=True, stop=True).then_inc(s_t2, 1)

                    def stats(n, par_):
                        wait(pe, s_tv, n * STAT_STEPS)
                        pe.wait_ge(s_mm, n * NG + NG)
                        pe.wait_ge(s_sq, n * NG + NG)
                        nc.tensor.matmul(pst[:, 0:32], ones, stat[:, 0:32], start=True, stop=True)
                        nc.tensor.matmul(pst[0:32, 128:256], stat[:, 32:64], ident, start=True, stop=True)\
                            .then_inc(s_t1, 1)

                    def measure(n, k, r):
                        w = wsum[r][k % 2]
                        dst = psm[SCALES.index(r) % 2]
                        band = {key[1:]: const(C_BAND + v * P, P, P) for key, v in BAND_FOR.items() if key[0] == r}
                        rhs = {"even": cols(w, 0, NW)[:, 0, :], "odd": cols(w, 0, NW)[:, 1, :],
                               "pair": pair[r][:, :]}
                        c = n * NG + k
                        pe.wait_ge(s_w[r], c + 1)
                        before = {2: (8, 0), 4: (16, 0), 8: (2, 1), 16: (4, 1)}[r]
                        wait(pe, s_l[before[0]], c + before[1])
                        for e in (0, 1):
                            keys = [key for key in band if key[0] == e]
                            if e == 1 and r > 2:
                                pe.wait_ge(s_pr[r], c + 1)
                            for j, key in enumerate(keys):
                                last = nc.tensor.matmul(dst[:, e, :], band[key], rhs[key[1]],
                                                        start=(j == 0), stop=(j == len(keys) - 1))
                        last.then_inc(s_ms[r], 1)

                    def step(n, par_, k, entering, before, after):
                        if entering:
                            columns(*entering[0])
                        measure(n, k, 2)
                        if k == STATS_AT + 1 and after:
                            spread(after[0])
                        if entering:
                            rows(*entering[0])
                        measure(n, k, 4)
                        if len(entering) > 1:
                            columns(*entering[1])
                        measure(n, k, 8)
                        if len(entering) > 1:
                            rows(*entering[1])
                        measure(n, k, 16)

                    walk(pe, enter, lambda n, par_, k: spread(n), step, stats)

                @block.scalar
                def _(act):
                    act.wait_ge(s_pv, 1)
                    nc.scalar.activation(par[:, 0, :], raw[:, 3, :], ACT.Ln).then_inc(s_pa, 1)
                    act.wait_ge(s_pa, 1)
                    nc.scalar.activation(par[:, 0, :], par[:, 0, :], ACT.Exp, scale=-0.5).then_inc(s_pa, 1)
                    act.wait_ge(s_pad, 3)

                    def keep(n, par_, g):
                        act.wait_ge(s_u, n * NG + (g + 1))
                        wait(act, s_y, n * NG + (g - 1))
                        nc.scalar.activation(usb[g % 2][:, :].rearrange("p (w c) -> p c w", c=GC),
                                             psu[0:K0, :].rearrange("p (c w) -> p c w", c=GC),
                                             ACT.Copy).then_inc(s_us, 1)

                    def square(n, par_, g):
                        act.wait_ge(s_x1, n * NG + (g + 1))
                        if g == 0:
                            wait(act, s_t1, n)
                        wait(act, s_sq, n * NG + g)
                        nc.scalar.activation(as2(junk[:, :]), group(par_, g), ACT.Square,
                                             accum_out=stat[:, NG + g:NG + g + 1]).then_inc(s_sq, 1)

                    def enter(n, par_, g):
                        keep(n, par_, g)
                        square(n, par_, g)

                    def roots(n):
                        act.wait_ge(s_tv, n * STAT_STEPS + 9)
                        nc.scalar.activation(sm[:, 4, :], sm[:, 3, :], ACT.Ln).then_inc(s_ta, 1)
                        act.wait_ge(s_ta, n * 2 + 1)
                        nc.scalar.activation(sm[:, 4, :], sm[:, 4, :], ACT.Exp, scale=-0.5).then_inc(s_ta, 1)

                    def prepare(n, par_, k):
                        roots(n)
                        scaled(n, par_, k)

                    def scaled(n, par_, k):
                        if k == 0:
                            act.wait_ge(s_tv, n * STAT_STEPS + STAT_STEPS)
                        wait(act, s_w[2], n * NG + k)
                        nc.scalar.activation(
                            cols(xn, 0, NW).rearrange("p q (w c) -> p q w c", c=GC),
                            group(par_, k).rearrange("p (q w) c -> p q w c", q=2),
                            ACT.Relu, scale=aff[:, par_, 0, k:k + 1], bias=aff[:, par_, 1, k:k + 1])\
                            .then_inc(s_xn, 1)

                    def log(n, par_, k, r):
                        dst = logs[r][k % 2]
                        c = n * NG + k
                        if r == 2:
                            wait(act, s_lo, c)
                        elif r == 4:
                            wait(act, s_t, c)
                        elif r == 8:
                            wait(act, s_o, c - 1)
                        else:
                            wait(act, s_f, c)
                        if r == 2:
                            act.wait_ge(s_pr[2], c + 1)
                            nc.scalar.activation(dst[:, 0:NPX], pair[2][:, :], ACT.Ln, bias=eps_k)
                            act.wait_ge(s_ms[2], c + 1)
                            nc.scalar.activation(dst[:, NPX:2 * NPX], psm[0][:, 1, :], ACT.Ln,
                                                 bias=eps_k).then_inc(s_l[2], 1)
                        else:
                            act.wait_ge(s_ms[r], c + 1)
                            nc.scalar.activation(
                                dst[:, :], psm[SCALES.index(r) % 2][:, :, :].rearrange("p e m -> p (e m)"),
                                ACT.Ln, bias=eps_k).then_inc(s_l[r], 1)

                    def step(n, par_, k, entering, before, after):
                        if before:
                            log(*before, 16)
                        new = after and after[2] == 0
                        if after and not new:
                            scaled(*after)
                        if entering:
                            keep(*entering[0])
                        log(n, par_, k, 2)
                        if new:
                            roots(after[0])
                        if entering:
                            square(*entering[0])
                        log(n, par_, k, 4)
                        if new:
                            scaled(*after)
                        if len(entering) > 1:
                            keep(*entering[1])
                        log(n, par_, k, 8)
                        if len(entering) > 1:
                            square(*entering[1])

                    walk(act, enter, prepare, step, lambda *a: None, lambda *a: log(*a, 16))

                @block.vector
                def _(dve):
                    steps = [0]

                    def plink(ins):
                        steps[0] += 1
                        ins.then_inc(s_pv, 1)
                        dve.wait_ge(s_pv, steps[0])

                    nc.vector.memset(eps_k, EPS_K).then_inc(s_pad, 1)
                    nc.vector.memset(xn[:, :, :], 0.0).then_inc(s_pad, 1)
                    nc.vector.memset(vin[:, :, :], 0.0).then_inc(s_pad, 1)
                    dve.wait_ge(s_par, 64)
                    ga, be, mm_, va = (raw[:, j, :] for j in range(4))
                    kc, dc = par[:, 0, :], par[:, 1, :]
                    plink(nc.vector.tensor_scalar(va, va, EPS_BN, None, ALU.add))
                    dve.wait_ge(s_pa, 2)
                    plink(nc.vector.tensor_tensor(dc, kc, kc, ALU.mult))
                    plink(nc.vector.tensor_tensor(dc, dc, va, ALU.mult))
                    plink(nc.vector.tensor_scalar(dc, dc, -0.5, 1.5, ALU.mult, ALU.add))
                    plink(nc.vector.tensor_tensor(kc, kc, dc, ALU.mult))
                    plink(nc.vector.tensor_tensor(kc, kc, ga, ALU.mult))
                    plink(nc.vector.tensor_tensor(dc, kc, mm_, ALU.mult))
                    plink(nc.vector.tensor_tensor(dc, be, dc, ALU.subtract))
                    plink(nc.vector.tensor_scalar(kc, kc, 1.0 / (10.0 * LN2), None, ALU.mult))
                    assert steps[0] == PARAM_STEPS

                    def add(n, par_, g):
                        if g == 0:
                            wait(dve, s_x[par_], n * 8 - 8 * par_ + 16 * par_)
                            wait(dve, s_t1, n)
                        dve.wait_ge(s_y, n * NG + (g + 1))
                        nc.vector.scalar_tensor_tensor(
                            group(par_, g), group(par_, g), 1.0,
                            as2(psy[:, :, :].rearrange("p q m -> p (q m)")), ALU.mult, ALU.add,
                            accum_out=stat[:, g:g + 1]).then_inc(s_x1, 1)

                    def extrema(n, par_, g):
                        dve.wait_ge(s_x1, n * NG + (g + 1))
                        for j, op in ((2, ALU.min), (3, ALU.max)):
                            last = nc.vector.tensor_reduce(stat[:, j * NG + g:j * NG + g + 1],
                                                           group(par_, g), mybir.AxisListType.XY, op)
                        last.then_inc(s_mm, 1)

                    def enter(n, par_, g):
                        add(n, par_, g)
                        extrema(n, par_, g)

                    def linker(n, done):
                        def link(ins):
                            done[0] += 1
                            ins.then_inc(s_tv, 1)
                            dve.wait_ge(s_tv, n * STAT_STEPS + done[0])
                        return link

                    mean, ex2, t, ve, r0, s, lo, hi = (sm[:, j, :] for j in range(8))

                    def stats(n, par_):
                        k = [0]
                        link = linker(n, k)
                        dve.wait_ge(s_t1, n + 1)
                        ext = pst[0:32, 128:256]
                        link(nc.vector.tensor_reduce(red[:, 0:1], ext, X_AXIS, ALU.min))
                        link(nc.vector.tensor_reduce(red[:, 1:2], ext, X_AXIS, ALU.max))
                        for j in range(2):
                            link(nc.vector.tensor_scalar(diag[:, 32 * j:32 * j + 32], ident[0:32, 0:32],
                                                         red[:, j:j + 1], None, ALU.mult))
                        link(nc.vector.tensor_scalar(mean, pst[:, 0:16], 1.0 / GROUP, None, ALU.mult))
                        link(nc.vector.tensor_scalar(ex2, pst[:, 16:32], 1.0 / GROUP, None, ALU.mult))
                        link(nc.vector.tensor_tensor(t, mean, mean, ALU.mult))
                        link(nc.vector.tensor_tensor(ve, ex2, t, ALU.subtract))
                        link(nc.vector.tensor_scalar(ve, ve, 0.0, EPS_GN, ALU.max, ALU.add))
                        assert k[0] == 9, k[0]

                    def stats_end(n, par_):
                        k = [9]
                        link = linker(n, k)
                        dve.wait_ge(s_ta, n * 2 + 2)
                        link(nc.vector.tensor_tensor(t, r0, r0, ALU.mult))
                        link(nc.vector.tensor_tensor(t, t, ve, ALU.mult))
                        link(nc.vector.tensor_scalar(t, t, -0.5, 1.5, ALU.mult, ALU.add))
                        link(nc.vector.tensor_tensor(s, r0, t, ALU.mult))
                        dve.wait_ge(s_t2, n + 1)
                        link(nc.vector.tensor_tensor(lo, pst[:, 256:272], mean, ALU.subtract))
                        link(nc.vector.tensor_tensor(lo, lo, s, ALU.mult))
                        link(nc.vector.tensor_tensor(hi, pst[:, 304:320], mean, ALU.subtract))
                        link(nc.vector.tensor_tensor(hi, hi, s, ALU.mult))
                        mn, mx, inv = sc1[:, 0:1], sc1[:, 1:2], sc1[:, 2:3]
                        link(nc.vector.tensor_reduce(mn, lo, X_AXIS, ALU.min))
                        link(nc.vector.tensor_reduce(mx, hi, X_AXIS, ALU.max))
                        link(nc.vector.tensor_tensor(mx, mx, mn, ALU.subtract))
                        link(nc.vector.tensor_scalar(mx, mx, EPS_K, None, ALU.add))
                        link(nc.vector.reciprocal(inv, mx))
                        link(nc.vector.tensor_tensor(t, mean, s, ALU.mult))
                        link(nc.vector.tensor_scalar(t, t, mn, -1.0, ALU.add, ALU.mult))
                        link(nc.vector.tensor_scalar(aff[:, par_, 0, :], s, inv, None, ALU.mult))
                        link(nc.vector.tensor_scalar(aff[:, par_, 1, :], t, inv, None, ALU.mult))
                        assert k[0] == STAT_STEPS, k[0]

                    def sums(n, k, r):
                        w0, m = SPAN[r]
                        c = n * NG + k
                        if r == 2:
                            dve.wait_ge(s_xn, c + 1)
                            a, b = cols(xn, w0, m), cols(xn, w0 + 1, m)
                        else:
                            src, d = wsum[r // 2][k % 2], STEP[r]
                            dve.wait_ge(s_w[r // 2], c + 1)
                            a, b = cols(src, w0 - d, m), cols(src, w0 + d, m)
                        back = 2 if r < 8 else 1
                        wait(dve, s_ms[r], c + (1 - back))
                        if r > 2:
                            wait(dve, s_pr[r], c + (1 - back))
                        if r == 8:
                            wait(dve, s_w[16], c)
                        nc.vector.tensor_tensor(cols(wsum[r][k % 2], w0, m), a, b, ALU.add).then_inc(s_w[r], 1)

                    def pair2(n, k):
                        c = n * NG + k
                        dve.wait_ge(s_w[2], c + 1)
                        wait(dve, s_l[2], c)
                        w = cols(wsum[2][k % 2], 0, NW)
                        nc.vector.tensor_tensor(pair[2][:, :], w[:, 0, :], w[:, 1, :], ALU.add)\
                            .then_inc(s_pr[2], 1)

                    def pairs(n, k, r):
                        c = n * NG + k
                        dve.wait_ge(s_w[r], c + 1)
                        wait(dve, s_ms[r], c)
                        w = cols(wsum[r][k % 2], 0, NW)
                        nc.vector.tensor_tensor(pair[r][:, :], w[:, 0, :], w[:, 1, :], ALU.add)\
                            .then_inc(s_pr[r], 1)

                    def prepare(n, par_, k):
                        stats_end(n, par_)
                        sums(n, k, 2)
                        pair2(n, k)
                        sums(n, k, 4)
                        sums(n, k, 8)

                    def lower(n, k):
                        l2, l4 = logs[2][0][:, :], logs[4][0][:, :]
                        dve.wait_ge(s_l[2], n * NG + (k + 1))
                        dve.wait_ge(s_l[4], n * NG + (k + 1))
                        nc.vector.scalar_tensor_tensor(l2, l2, 3.0, l4, ALU.mult, ALU.add).then_inc(s_t, 1)

                    def exponent(n, par_, k):
                        l8, l16 = logs[8][k % 2][:, :], logs[16][0][:, :]
                        dve.wait_ge(s_lo, n * NG + (k + 1))
                        dve.wait_ge(s_l[16], n * NG + (k + 1))
                        nc.vector.scalar_tensor_tensor(l8, l16, 3.0, l8, ALU.mult, ALU.add).then_inc(s_f, 1)

                    def output(n, par_, k):
                        dve.wait_ge(s_f, n * NG + (k + 1))
                        dve.wait_ge(s_xd, n * NG + (k + 1))
                        for c in range(GC):
                            dst = group(par_, k)[:, :, c]
                            last = nc.vector.scalar_tensor_tensor(
                                dst, as2(logs[8][k % 2][:, :])[:, :, c], kc[:, GC * k + c:GC * k + c + 1],
                                dst, ALU.mult, ALU.add)
                        last.then_inc(s_o, 1)

                    def step(n, par_, k, entering, before, after):
                        new = after and after[2] == 0
                        if after and not new:
                            sums(after[0], after[2], 2)
                        if before:
                            exponent(*before)
                        if after and not new:
                            pair2(after[0], after[2])
                        if before:
                            output(*before)
                        if new:
                            lower(n, k)
                            stats_end(after[0], after[1])
                            sums(after[0], after[2], 2)
                            pair2(after[0], after[2])
                        if entering:
                            add(*entering[0])
                        if after:
                            sums(after[0], after[2], 4)
                        if entering:
                            extrema(*entering[0])
                        if not new:
                            lower(n, k)
                        if len(entering) > 1:
                            add(*entering[1])
                        if after:
                            sums(after[0], after[2], 8)
                        if after and not entering:
                            pairs(after[0], after[2], 4)
                            pairs(after[0], after[2], 8)
                        if len(entering) > 1:
                            extrema(*entering[1])

                    def finish(n, par_, k):
                        exponent(n, par_, k)
                        output(n, par_, k)

                    walk(dve, enter, prepare, step, stats, finish)

                @block.gpsimd
                def _(pool):
                    pool.wait_ge(s_pv, PARAM_STEPS)

                    def pairs(n, k, r):
                        c = n * NG + k
                        pool.wait_ge(s_w[r], c + 1)
                        wait(pool, s_ms[r], c)
                        w = cols(wsum[r][k % 2], 0, NW)
                        nc.gpsimd.tensor_tensor(pair[r][:, :], w[:, 0, :], w[:, 1, :], ALU.add)\
                            .then_inc(s_pr[r], 1)

                    def sums16(n, k):
                        src, d = wsum[8][k % 2], STEP[16]
                        pool.wait_ge(s_w[8], n * NG + (k + 1))
                        wait(pool, s_ms[16], n * NG + k)
                        nc.gpsimd.tensor_tensor(cols(wsum[16][0], 0, NW), cols(src, -d, NW), cols(src, d, NW),
                                                ALU.add).then_inc(s_w[16], 1)

                    def shift(n, par_, k):
                        pool.wait_ge(s_xn, n * NG + (k + 1))
                        dc = par[:, 1:2, GC * k:GC * (k + 1)].broadcast_to([P, 2 * NW, GC])
                        nc.gpsimd.tensor_tensor(group(par_, k), group(par_, k), dc, ALU.add)\
                            .then_inc(s_xd, 1)

                    def take_lower(n, k):
                        pool.wait_ge(s_t, n * NG + (k + 1))
                        pool.wait_ge(s_l[8], n * NG + (k + 1))
                        l8 = logs[8][k % 2][:, :]
                        nc.gpsimd.tensor_tensor(l8, l8, logs[2][0][:, :], ALU.subtract).then_inc(s_lo, 1)

                    def prepare(n, par_, k):
                        pairs(n, k, 4)
                        pairs(n, k, 8)

                    def step(n, par_, k, entering, before, after):
                        sums16(n, k)
                        pairs(n, k, 16)
                        shift(n, par_, k)
                        if after and entering:
                            pairs(after[0], after[2], 4)
                        take_lower(n, k)
                        if after and entering:
                            pairs(after[0], after[2], 8)

                    walk(pool, lambda *a: None, prepare, step, lambda *a: None)


SLOT_STEPS = 14
MID_STEPS = 10
PARAM_STEPS = 9
STAT_STEPS = 26

_INS = ["x", "L0_conv_w_re", "L0_conv_w_im", "L0_conv_idx0", "L0_conv_idx1", "L1_conv_gamma",
        "L1_conv_beta", "L1_conv_moving_mean", "L1_conv_moving_var"]


def kernel(**inputs):
    import concourse.bacc as _bacc
    from concourse.bass_utils import run_bass_kernel_spmd as _run

    nc = _bacc.Bacc("TRN2", target_bir_lowering=False, num_devices=1)
    arrays, args = {}, []
    for name in _INS:
        a = np.ascontiguousarray(inputs[name])
        arrays[f"in_{name}"] = a
        args.append(nc.dram_tensor(f"in_{name}", a.shape, mybir.dt.from_np(a.dtype), kind="ExternalInput").ap())
    table = constants()
    arrays["in_table"] = table
    args.append(nc.dram_tensor("in_table", table.shape, F32, kind="ExternalInput").ap())
    args.append(nc.dram_tensor("out_0", (NB, NH, NW, NC), F32, kind="ExternalOutput").ap())
    build(nc, *args)
    r = _run(nc, [arrays], core_ids=[0])
    return r.results[0]["out_0"]
```

```python
from contextlib import ExitStack

import numpy as np

import concourse.bass as bass
from concourse import mybir

F32 = mybir.dt.float32
BF16 = mybir.dt.bfloat16
I32 = mybir.dt.int32
ALU = mybir.AluOpType
ACT = mybir.ActivationFunctionType
X_AXIS = mybir.AxisListType.X

P = 128
NB = 16
NH = NW = 256
NC = 32
NG = 16
GC = NC // NG
NM = 415
KMAX = 16
K1 = KMAX + 1
K0 = 2 * KMAX + 1
NSLOT = K0 * K1
PIX = NH * NW
GROUP = PIX * GC
EPS_GN = 1e-5
EPS_K = 1e-7
EPS_BN = 1e-3
SCALES = (2, 4, 8, 16)
LN2 = float(np.log(2.0))

BAND_FOR = {}
for _r in SCALES:
    if _r == 2:
        _list = [(2, 1, "odd"), (2, 1, "even")]
    else:
        _list = [(_r, 1, "pair"), (_r, 0, "shifted")]
    for _k in _list:
        BAND_FOR[_k] = len(BAND_FOR)
C_BAND = 0
C_IDENT = C_BAND + P * len(BAND_FOR)
C_ONES = C_IDENT + P
C_BH = C_ONES + P
C_FI = C_BH + 2 * P
C_KEEP = C_FI + NW
C_BF = C_KEEP
C_FB = C_BF + 2 * K0
C_CEN = C_FB + 4 * 4 * K1
C_PAIR = C_CEN + 64
C_GRP = C_PAIR + 64
C_SEL = C_GRP + 64
C_END = C_SEL + 4 * P


def constants():
    t = np.zeros((P, C_END), np.float64)
    p = np.arange(P)
    for (r, e, src), i in BAND_FOR.items():
        out_row = 2 * p[None, :] + e
        lo, hi = out_row - (r // 2 - 1), out_row + r // 2
        if src in ("pair", "shifted"):
            first = 2 * p[:, None] + (src == "shifted")
            band = (first >= lo) & (first + 1 <= hi)
        else:
            row = 2 * p[:, None] + (src == "odd")
            band = (row >= lo) & (row <= hi)
        t[:, C_BAND + i * P:C_BAND + (i + 1) * P] = band
    t[:, C_IDENT:C_IDENT + P] = np.eye(P)
    t[:, C_ONES:C_ONES + P] = 1.0
    turn = 2 * np.pi / NH
    k1 = np.arange(K1)
    for q in range(2):
        h = 2 * p + q
        for a in range(1, KMAX + 1):
            t[a, C_BH + q * P:C_BH + (q + 1) * P] = np.sin(turn * (a * h % NH))
            t[K1 + a - 1, C_BH + q * P:C_BH + (q + 1) * P] = np.cos(turn * (a * h % NH))
            t[:, C_BF + q * K0 + 2 * a - 1] = np.cos(turn * (a * h % NH))
            t[:, C_BF + q * K0 + 2 * a] = np.sin(turn * (a * h % NH))
        t[0, C_BH + q * P:C_BH + (q + 1) * P] = 1.0
        t[:, C_BF + q * K0] = 1.0
    weight = np.where(k1 == 0, 1.0, 2.0) / PIX
    ang = turn * (k1[:, None] * np.arange(NW)[None, :] % NW)
    t[0:K1, C_FI:C_FI + NW] = weight[:, None] * np.cos(ang)
    t[32:32 + K1, C_FI:C_FI + NW] = weight[:, None] * np.sin(ang)
    for v in range(2):
        ang = turn * ((P * v + p)[:, None] * k1[None, :] % NW)
        c, s = np.cos(ang), np.sin(ang)
        at = C_FB + v * 8 * K1
        t[:, at:at + 4 * K1] = np.concatenate([c, -s, c, -s], 1)
        t[:, at + 4 * K1:at + 8 * K1] = np.concatenate([-s, -c, s, c], 1)
    e = np.eye(32)
    pair = np.kron(np.eye(NG), np.full((GC, GC), 1.0 / GC))
    t[0:32, C_CEN:C_CEN + 32] = e - pair
    t[32:64, C_CEN + 32:C_CEN + 64] = e
    t[0:32, C_PAIR:C_PAIR + 32] = pair / PIX
    t[0:32, C_PAIR + 32:C_PAIR + 64] = pair / PIX
    spread = np.kron(np.eye(NG), np.ones((1, GC))) / GROUP
    t[0:NG, C_GRP:C_GRP + 32] = spread
    t[0:NG, C_GRP + 32:C_GRP + 64] = spread
    for i, r in enumerate(SCALES[1:]):
        for k in range(96):
            at = C_SEL + i * P + 4 * (k % 32)
            t[k, at:at + r // 4] = 1.0
    return t.astype(np.float32)


ENTER = {k: [] for k in range(NG)}
for _g in range(NG):
    ENTER[6 + _g // 3 if _g < 12 else 10 + (_g - 12) // 2].append(_g)
STATS_AT = 12

LO, HI = 7, 8
WP = NW + LO + HI
SPAN = {2: (-7, 270), 4: (-6, 268), 8: (-4, 264), 16: (0, 256)}
STEP = {4: 1, 8: 2, 16: 4}


def build(nc, x, w_re, w_im, idx0, idx1, gamma, beta, mov_mean, mov_var, table, out):
    ctx = ExitStack()
    with ctx:
        def sb(name, shape, dt=F32):
            return ctx.enter_context(nc.sbuf_tensor(name, shape, dt))

        def sem(name):
            return ctx.enter_context(nc.semaphore(name))

        wtab = nc.dram_tensor("wtab", [NSLOT + 1, 64, 64], F32, kind="Internal").ap()
        vtab = [nc.dram_tensor("vtab_even", [2, K1 * K1, NB, NC], F32, kind="Internal").ap(),
                nc.dram_tensor("vtab_odd", [2, KMAX * K1, NB, NC], F32, kind="Internal").ap()]

        arena = sb("arena", [P, 2 * 2 * NW * NC])
        cst = sb("cst", [P, C_KEEP])
        sel = sb("sel", [96, 4, P], BF16)
        ssqb = sb("ssqb", [NG, NB])
        half = NW * NC
        xbuf = [arena[:, n * 2 * half:(n + 1) * 2 * half] for n in range(2)]

        early = ExitStack()
        cst1 = early.enter_context(nc.sbuf_tensor("cst1", [P, C_END - C_KEEP], F32))

        def const(at, rows, cols):
            if at >= C_KEEP:
                return cst1[0:rows, at - C_KEEP:at - C_KEEP + cols]
            return cst[0:rows, at:at + cols]

        def wait(eng, semaphore, count):
            if not isinstance(count, int) or count > 0:
                eng.wait_ge(semaphore, count)

        ident = const(C_IDENT, P, P)
        ones = const(C_ONES, P, P)

        with ExitStack() as one:
            def psum1(name, shape):
                return one.enter_context(nc.psum_tensor(name, shape, F32))

            psr = psum1("psr", [P, 2, 512])
            psz = psum1("psz", [P, 2, 512])
            psx = psum1("psx", [P, 3, 512])
            pss = psum1("pss", [P, 512])
            xh = [arena[:, v * half:(v + 1) * half].rearrange("p (q w c) -> p q w c", q=2, w=P)
                  for v in range(2)]
            at = 2 * half
            modes_all = arena[:, at:at + NSLOT * NB].rearrange("p (s b) -> p s b", b=NB)
            modes = modes_all[0:64]
            at += NSLOT * NB
            zsb = arena[:, at:at + 2 * K0 * NC].rearrange("p (v k c) -> p v k c", v=2, k=K0)
            at += 2 * K0 * NC
            wrow = arena[0:83, 4 * half - 4096:4 * half].rearrange("p (i o) -> p i o", i=64)
            assert at <= 4 * half - 4096
            rsb = [one.enter_context(nc.sbuf_tensor(f"rsb{v}", [P, P * NC], F32)) for v in range(2)]
            NJ = 4
            junk1 = one.enter_context(nc.sbuf_tensor("junk1", [P, 2, NJ, 512], BF16))
            ssq1 = one.enter_context(nc.sbuf_tensor("ssq1", [P, 2, NG], F32))
            zero = one.enter_context(nc.sbuf_tensor("zero", [P, 1024], F32))
            wraw = one.enter_context(nc.sbuf_tensor("wraw", [83, 2, NC * NC], F32))
            idx = one.enter_context(nc.sbuf_tensor("idx", [83, 2, 5], I32))
            sl = one.enter_context(nc.sbuf_tensor("sl", [83, 6, 5], F32))
            slot = one.enter_context(nc.sbuf_tensor("slot", [83, 5], I32))

            s_cst = sem("consts_in")
            s_xin = [sem(f"x_half_in{v}") for v in range(2)]
            s_xsq = [sem(f"x_half_squared{v}") for v in range(2)]
            s_r = [sem(f"rows_done{v}") for v in range(2)]
            s_re = [sem(f"rows_kept{v}") for v in range(2)]
            s_rz = sem("row_zeros_set")
            s_z = [sem(f"columns_turned{v}") for v in range(2)]
            s_ze = [sem(f"columns_kept{v}") for v in range(2)]
            s_m = [sem(f"modes_done{k}") for k in range(3)]
            s_me = [sem(f"modes_kept{k}") for k in range(3)]
            s_ss = sem("squares_summed")
            s_sse = sem("squares_kept")
            s_idx = sem("indices_in")
            s_sl = sem("slot_steps")
            s_zero = sem("zero_set")
            s_clear = sem("table_cleared")
            s_wrow = sem("weight_rows_built")
            s_wraw = sem("weights_raw_in")
            s_scat = sem("weight_rows_out")
            s_mzero = sem("mode_zeros_set")

            NR = P * NC // 512
            NT = NC // 8
            XA = [(0, 15), (15, 14), (29, 4)]
            xv = x.rearrange("b (p q) (v w) c -> b v p q (w c)", q=2, v=2)

            with nc.Block() as block:
                @block.sync
                def _(sync):
                    sync.dma_start(cst[:, :], table[:, 0:C_KEEP]).then_inc(s_cst, 16)
                    sync.dma_start(cst1[:, :], table[:, C_KEEP:C_END]).then_inc(s_cst, 16)

                    def load(n):
                        for v in range(2):
                            wait(sync, s_xsq[v], n * NG)
                            wait(sync, s_r[v], n * 2 * NR)
                            sync.dma_start(xh[v].rearrange("p q w c -> p q (w c)"),
                                           xv[bass.ds(n, 1), v].rearrange("b p q m -> (b p) q m"))\
                                .then_inc(s_xin[v], 16)

                    load(0)
                    with sync.Fori(1, NB) as n:
                        load(n)

                @block.gpsimd
                def _(pool):
                    pool.memset(zero[:, :], 0.0).then_inc(s_zero, 1)
                    pool.dma_start(idx[:, 0, :], idx0.rearrange("(p t) -> p t", p=83)).then_inc(s_idx, 16)
                    pool.dma_start(idx[:, 1, :], idx1.rearrange("(p t) -> p t", p=83)).then_inc(s_idx, 16)
                    pool.wait_ge(s_zero, 1)
                    flat = wtab.rearrange("s i o -> s (i o)")
                    done = 0
                    while done < NSLOT + 1:
                        k = min(P, NSLOT + 1 - done)
                        pool.dma_start(flat[done:done + k, :].rearrange("s (r m) -> s r m", r=4),
                                       zero[0:k, :].rearrange("p (r m) -> p r m", r=1).broadcast_to([k, 4, 1024]))\
                            .then_inc(s_clear, 16)
                        done += k
                    pool.wait_ge(s_clear, 16 * 5)
                    pool.wait_ge(s_sl, SLOT_STEPS)
                    for t in range(5):
                        for j, w in enumerate((w_re, w_im)):
                            pool.dma_start(wraw[:, j], w.rearrange("(p t) i o -> t p (i o)", p=83)[t])\
                                .then_inc(s_wraw, 16)
                        if t:
                            pool.wait_ge(s_scat, 16 * t)
                        pool.wait_ge(s_wraw, 32 * (t + 1))
                        re, im = (wraw[:, j, :].rearrange("p (i o) -> p i o", i=NC) for j in range(2))
                        pool.tensor_copy(wrow[:, 0:32, 0:32], re).then_inc(s_wrow, 1)
                        pool.tensor_copy(wrow[:, 0:32, 32:64], im).then_inc(s_wrow, 1)
                        pool.tensor_copy(wrow[:, 32:64, 32:64], re).then_inc(s_wrow, 1)
                        pool.tensor_scalar(wrow[:, 32:64, 0:32], im, -1.0, None, ALU.mult).then_inc(s_wrow, 1)
                        pool.wait_ge(s_wrow, 4 * (t + 1))
                        pool.indirect_dma_start(
                            flat, bass.IndirectOffsetOnAxis(ap=slot[:, t:t + 1], axis=0),
                            wrow.rearrange("p i o -> p (i o)"), None).then_inc(s_scat, 16)
                    pool.wait_ge(s_scat, 16 * 5)

                @block.scalar
                def _(act):
                    def squares(n):
                        for v in range(2):
                            act.wait_ge(s_xin[v], n * 16 + 16)
                            if v == 0:
                                wait(act, s_ss, n)
                            for g in range(NG):
                                wait(act, s_xsq[v], n * NG + max(g - NJ + 1, 0))
                                nc.scalar.activation(
                                    junk1[:, v, g % NJ, :].rearrange("p (w c) -> p w c", c=GC),
                                    xh[v].rearrange("p q w c -> p (q w) c")[:, :, GC * g:GC * (g + 1)],
                                    ACT.Square, accum_out=ssq1[:, v, g:g + 1]).then_inc(s_xsq[v], 1)

                    squares(0)
                    with act.Fori(1, NB) as n:
                        squares(n)

                @block.vector
                def _(dve):
                    nc.vector.memset(modes_all[64:128], 0.0).then_inc(s_mzero, 1)
                    dve.wait_ge(s_cst, 32)
                    nc.vector.tensor_copy(sel[:, :, :].rearrange("p a m -> p (a m)"), const(C_SEL, 96, 4 * P))
                    steps = [0]

                    def link(ins):
                        steps[0] += 1
                        ins.then_inc(s_sl, 1)
                        dve.wait_ge(s_sl, steps[0])

                    dve.wait_ge(s_idx, 32)
                    k0, k1, hi, t0, t1, t2 = (sl[:, j, :] for j in range(6))
                    link(nc.vector.tensor_copy(k0, idx[:, 0, :]))
                    link(nc.vector.tensor_copy(k1, idx[:, 1, :]))
                    link(nc.vector.tensor_scalar(hi, k0, float(NH // 2), -float(NH), ALU.is_ge, ALU.mult))
                    link(nc.vector.tensor_tensor(k0, k0, hi, ALU.add))
                    link(nc.vector.tensor_scalar(hi, k0, 0.0, None, ALU.is_gt))
                    link(nc.vector.tensor_scalar(t0, k0, -1.0, None, ALU.mult))
                    link(nc.vector.tensor_tensor(t0, k0, t0, ALU.max))
                    link(nc.vector.tensor_tensor(t1, t0, k1, ALU.max))
                    link(nc.vector.tensor_scalar(t1, t1, float(KMAX), float(2 * NSLOT), ALU.is_gt, ALU.mult))
                    link(nc.vector.scalar_tensor_tensor(t2, hi, float(KMAX), t0, ALU.mult, ALU.add))
                    link(nc.vector.scalar_tensor_tensor(t2, t2, float(K1), k1, ALU.mult, ALU.add))
                    link(nc.vector.tensor_tensor(t2, t2, t1, ALU.add))
                    link(nc.vector.tensor_scalar(t2, t2, float(NSLOT), None, ALU.min))
                    link(nc.vector.tensor_copy(slot[:, :], t2))
                    assert steps[0] == SLOT_STEPS

                    def keep(n):
                        for v in range(2):
                            for i in range(NR):
                                dve.wait_ge(s_r[v], n * 2 * NR + 2 * (i + 1))
                                if i == 0:
                                    wait(dve, s_z[v], n * NT)
                                nc.vector.tensor_copy(rsb[v][0:K0, i * 512:(i + 1) * 512], psr[0:K0, i % 2, :])\
                                    .then_inc(s_re[v], 1)
                            if v == 0 and not (isinstance(n, int) and n == 0):
                                keep_modes(n - 1)
                            for i in range(NT):
                                dve.wait_ge(s_z[v], n * NT + (i + 1))
                                nc.vector.tensor_copy(
                                    zsb[:, v, :, i * 8:(i + 1) * 8].rearrange("p k c -> p c k"),
                                    psz[:, i % 2, 0:8 * K0].rearrange("p (c k) -> p c k", c=8))\
                                    .then_inc(s_ze[v], 1)

                    def keep_modes(n):
                        for k, (j0, m) in enumerate(XA):
                            dve.wait_ge(s_m[k], n + 1)
                            for ri in range(2):
                                out_rows = modes[32 * ri:32 * ri + 32]
                                bank = psx[0:32, k, 0:m * 2 * K1].rearrange("p (j r f) -> p j r f", j=m, r=2)
                                if k == 0:
                                    nc.vector.tensor_copy(
                                        out_rows[:, 0:K1, bass.ds(n, 1)].rearrange("p f b -> p (f b)"),
                                        bank[:, 0, ri, :])
                                a0, na, skip = (j0 + 1 if k else 2) // 2, m // 2, m % 2
                                for sign in range(2):
                                    s0 = (a0 + KMAX * (1 - sign)) * K1
                                    last = nc.vector.tensor_copy(
                                        out_rows[:, s0:s0 + na * K1, bass.ds(n, 1)]
                                        .rearrange("p (a f) b -> p a (f b)", a=na),
                                        bank[:, skip + sign::2, ri, :])
                            last.then_inc(s_me[k], 1)
                        dve.wait_ge(s_ss, n + 1)
                        nc.vector.tensor_copy(ssqb[:, bass.ds(n, 1)], pss[0:NG, 0:1]).then_inc(s_sse, 1)

                    nc.vector.memset(rsb[0][:, :], 0.0).then_inc(s_rz, 1)
                    nc.vector.memset(rsb[1][:, :], 0.0).then_inc(s_rz, 1)
                    dve.wait_ge(s_rz, 2)
                    keep(0)
                    with dve.Fori(1, NB) as n:
                        keep(n)
                    keep_modes(NB - 1)

                @block.tensor
                def _(pe):
                    pe.wait_ge(s_cst, 32)
                    def over_rows(n, v):
                        pe.wait_ge(s_xin[v], n * 16 + 16)
                        flat = xh[v].rearrange("p q w c -> p q (w c)")
                        for i in range(NR):
                            if i >= 2:
                                pe.wait_ge(s_re[v], n * NR + (i - 1))
                            elif v == 1:
                                pe.wait_ge(s_re[0], n * NR + (NR - 1 + i))
                            else:
                                wait(pe, s_re[1], n * NR + (i - 1) if not isinstance(n, int) or n else 0)
                            for q in range(2):
                                nc.tensor.matmul(psr[0:K0, i % 2, :], const(C_BF + q * K0, P, K0),
                                                 flat[:, q, i * 512:(i + 1) * 512],
                                                 start=(q == 0), stop=(q == 1)).then_inc(s_r[v], 1)

                    def turn(n, v):
                        pe.wait_ge(s_re[v], n * NR + NR)
                        w_last = rsb[v][:, :].rearrange("p (w c) -> p w c", c=NC)
                        for i in range(NT):
                            if i >= 2:
                                pe.wait_ge(s_ze[v], n * NT + (i - 1))
                            elif v == 1:
                                pe.wait_ge(s_ze[0], n * NT + (NT - 1 + i))
                            else:
                                wait(pe, s_ze[1], n * NT + (i - 1) if not isinstance(n, int) or n else 0)
                            nc.tensor.transpose(psz[:, i % 2, 7 * K0:7 * K0 + P],
                                                w_last[:, :, i * 8 + 7], ident)
                            for c in range(7):
                                last = nc.tensor.transpose(psz[:, i % 2, c * K0:(c + 1) * K0],
                                                           w_last[0:K0, :, i * 8 + c], ident[0:K0, 0:K0])
                            last.then_inc(s_z[v], 1)

                    def transform(n):
                        if not (isinstance(n, int) and n == 0):
                            over_squares(n - 1)
                        for v in range(2):
                            over_rows(n, v)
                            if v == 0 and not (isinstance(n, int) and n == 0):
                                over_columns(n - 1)
                            turn(n, v)

                    def over_columns(n):
                        pe.wait_ge(s_ze[0], n * NT + NT)
                        pe.wait_ge(s_ze[1], n * NT + NT)
                        for k, (j0, m) in enumerate(XA):
                            wait(pe, s_me[k], n)
                            j = j0
                            while j < j0 + m:
                                cols = (4 if j else 2) * K1
                                comps = [(0, 0)] if j == 0 else [(j, 0), (j + 1, 1)]
                                ops = [(v, comp, kind) for comp, kind in comps for v in range(2)]
                                for i, (v, comp, kind) in enumerate(ops):
                                    last = nc.tensor.matmul(
                                        psx[0:32, k, (j - j0) * 2 * K1:(j - j0) * 2 * K1 + cols],
                                        zsb[:, v, comp, :],
                                        const(C_FB + v * 8 * K1 + kind * 4 * K1, P, cols),
                                        start=(i == 0), stop=(i == len(ops) - 1))
                                j += 2 if j else 1
                            last.then_inc(s_m[k], 1)

                    def over_squares(n):
                        for v in range(2):
                            pe.wait_ge(s_xsq[v], n * NG + NG)
                        wait(pe, s_sse, n)
                        for v in range(2):
                            last = nc.tensor.matmul(pss[0:NG, 0:1], ssq1[:, v, :], ones[:, 0:1],
                                                    start=(v == 0), stop=(v == 1))
                        last.then_inc(s_ss, 1)

                    transform(0)
                    with pe.Fori(1, NB) as n:
                        transform(n)
                    over_squares(NB - 1)
                    over_columns(NB - 1)

        with ExitStack() as mid:
            def psum2(name, shape):
                return mid.enter_context(nc.psum_tensor(name, shape, F32))

            psy = psum2("psymix", [P, 4, 512])
            psq = psum2("psq", [P, 4, 512])
            NWT = 3
            wt_all = mid.enter_context(nc.sbuf_tensor("wt", [P, NWT, K1, 64], F32))
            wt = [wt_all[:, j] for j in range(NWT)]
            BLOCKS = [(0, 0, 7), (0, 7, 7), (0, 14, 3), (1, 0, 7), (1, 7, 7), (1, 14, 2)]
            turned = mid.enter_context(nc.sbuf_tensor("turned", [P, len(BLOCKS), NB, 64], F32))
            st = mid.enter_context(nc.sbuf_tensor("st", [64, 6, NB], F32))

            s_st = sem("stat_matmuls")
            s_stv = sem("stat_steps")
            s_sta = sem("stat_logs")
            s_wt = [sem(f"weights_in{j}") for j in range(NWT)]
            s_mix = [sem(f"mixed{j}") for j in range(NWT)]
            s_mixe = [sem(f"mixed_kept{j}") for j in range(NWT)]
            s_yc = sem("modes_combined")
            s_v = [sem(f"turned{j}") for j in range(4)]
            s_vd = [sem(f"turned_kept_dve{j}") for j in range(4)]
            s_va = [sem(f"turned_kept_act{j}") for j in range(4)]
            s_vout = sem("parts_out")
            s_vz = sem("weight_zeros_set")
            s_x0 = sem("x_first_in")

            with nc.Block() as block:
                @block.sync
                def _(sync):
                    def load(buf, turn_no, j):
                        wait(sync, s_mix[buf], turn_no)
                        sync.dma_start(wt[buf][0:64], wtab[bass.ds(j * K1, K1)].rearrange("s i o -> i s o"))\
                            .then_inc(s_wt[buf], 16)

                    for buf, j in enumerate((0, K1, 1)):
                        load(buf, 0, j)
                    sync.dma_start(xbuf[0], x.rearrange("b (p q) w c -> b p (q w c)", q=2)[0])\
                        .then_inc(s_x0, 16)
                    with sync.Fori(1, KMAX) as a:
                        load(1, a, a + K1)
                        load(2, a, a + 1)
                    for i, (odd, j0, m) in enumerate(BLOCKS):
                        for j in range(2):
                            bank = (2 * i + j) % 4
                            turn_no = (2 * i + j) // 4 + 1
                            sync.wait_ge(s_vd[bank], turn_no)
                            sync.wait_ge(s_va[bank], turn_no)
                        r0 = j0 * K1
                        for part in range(2):
                            sync.dma_start(vtab[odd][part, r0:r0 + m * K1],
                                           turned[0:m * K1, i, :, part * NC:(part + 1) * NC])\
                                .then_inc(s_vout, 16)
                    sync.wait_ge(s_vout, 16 * 2 * len(BLOCKS))
                    sync.wait_ge(s_x0, 16)

                @block.scalar
                def _(act):
                    act.wait_ge(s_stv, 4)
                    nc.scalar.activation(st[:, 2, :], st[:, 1, :], ACT.Ln).then_inc(s_sta, 1)
                    act.wait_ge(s_sta, 1)
                    nc.scalar.activation(st[:, 2, :], st[:, 2, :], ACT.Exp, scale=-0.5).then_inc(s_sta, 1)
                    for i, (odd, j0, m) in enumerate(BLOCKS):
                        for j in range(2):
                            bank, turn_no = (2 * i + j) % 4, (2 * i + j) // 4 + 1
                            act.wait_ge(s_vd[bank], turn_no)
                            src = psq[0:m * K1, bank, :].rearrange("p (b o) -> p b o", b=8)
                            nc.scalar.activation(turned[0:m * K1, i, 8 * j:8 * j + 8, NC:2 * NC],
                                                 src[:, :, NC * odd:NC * odd + NC], ACT.Copy,
                                                 scale=-1.0 if odd else 1.0).then_inc(s_va[bank], 1)

                @block.vector
                def _(dve):
                    steps = [0]

                    def link(ins):
                        steps[0] += 1
                        ins.then_inc(s_stv, 1)
                        dve.wait_ge(s_stv, steps[0])

                    nc.vector.memset(wt_all[64:128], 0.0).then_inc(s_vz, 1)
                    dve.wait_ge(s_st, 1)
                    link(nc.vector.tensor_copy(st[:, 0, :], psy[0:64, 0, 0:NB]))
                    link(nc.vector.tensor_tensor(st[:, 0, :], st[:, 0, :], st[:, 0, :], ALU.mult))
                    link(nc.vector.tensor_tensor(st[:, 1, :], psy[0:64, 1, 0:NB], st[:, 0, :], ALU.subtract))
                    link(nc.vector.tensor_scalar(st[:, 1, :], st[:, 1, :], 0.0, EPS_GN, ALU.max, ALU.add))
                    dve.wait_ge(s_sta, 2)
                    link(nc.vector.tensor_tensor(st[:, 3, :], st[:, 2, :], st[:, 2, :], ALU.mult))
                    link(nc.vector.tensor_tensor(st[:, 3, :], st[:, 3, :], st[:, 1, :], ALU.mult))
                    link(nc.vector.tensor_scalar(st[:, 3, :], st[:, 3, :], -0.5, 1.5, ALU.mult, ALU.add))
                    link(nc.vector.tensor_tensor(st[:, 4, :], st[:, 3, :], st[:, 2, :], ALU.mult))
                    link(nc.vector.tensor_copy(modes[:, 0, :], psy[0:64, 2, 0:NB]))
                    link(nc.vector.tensor_tensor(
                        modes, modes, st[:, 4:5, :].broadcast_to([64, NSLOT, NB]), ALU.mult))

                    def slots(j, k):
                        return modes[:, bass.ds(j * K1, k * K1), :].rearrange("p s b -> p (s b)")

                    def mixed(j):
                        return psy[0:64, j, 0:K1 * NB]

                    dve.wait_ge(s_mix[0], 1)
                    zero_row = modes[:, 0:K1, :].rearrange("p s b -> p (s b)")
                    nc.vector.tensor_scalar(zero_row[0:32], mixed(0)[32:64], -1.0, None, ALU.mult)
                    nc.vector.tensor_copy(zero_row[32:64], mixed(0)[0:32]).then_inc(s_mixe[0], 1)
                    with dve.Fori(0, KMAX) as a:
                        dve.wait_ge(s_mix[1], a + 1)
                        nc.vector.tensor_copy(slots(a + K1, 1), mixed(1)).then_inc(s_mixe[1], 1)
                        dve.wait_ge(s_mix[2], a + 1)
                        dve.wait_ge(s_mixe[1], a + 1)
                        nc.vector.tensor_tensor(slots(a + 1, 1), mixed(2), slots(a + K1, 1), ALU.subtract)
                        nc.vector.tensor_tensor(slots(a + K1, 1), mixed(2), slots(a + K1, 1), ALU.add)\
                            .then_inc(s_mixe[2], 1)
                    for i, (odd, j0, m) in enumerate(BLOCKS):
                        for j in range(2):
                            bank, turn_no = (2 * i + j) % 4, (2 * i + j) // 4 + 1
                            dve.wait_ge(s_v[bank], turn_no)
                            src = psq[0:m * K1, bank, :].rearrange("p (b o) -> p b o", b=8)
                            nc.vector.tensor_copy(turned[0:m * K1, i, 8 * j:8 * j + 8, 0:NC],
                                                  src[:, :, NC * (1 - odd):NC * (1 - odd) + NC])\
                                .then_inc(s_vd[bank], 1)

                @block.tensor
                def _(pe):
                    nc.tensor.matmul(psy[0:64, 0, 0:NB], const(C_PAIR, 64, 64), modes[:, 0, :],
                                     start=True, stop=True)
                    nc.tensor.matmul(psy[0:64, 1, 0:NB], const(C_GRP, NG, 64), ssqb[:, :],
                                     start=True, stop=True)
                    nc.tensor.matmul(psy[0:64, 2, 0:NB], const(C_CEN, 64, 64), modes[:, 0, :],
                                     start=True, stop=True).then_inc(s_st, 1)
                    pe.wait_ge(s_stv, MID_STEPS)
                    pe.wait_ge(s_vz, 1)

                    def mix(buf, turn_no, j):
                        pe.wait_ge(s_wt[buf], turn_no * 16 + 16)
                        wait(pe, s_mixe[buf], turn_no)
                        for s in range(K1):
                            last = nc.tensor.matmul(
                                psy[0:64, buf, s * NB:(s + 1) * NB], wt[buf][:, s, :],
                                modes_all[:, bass.ds(j * K1 + s, 1), :].rearrange("p s b -> p (s b)"),
                                start=True, stop=True)
                        last.then_inc(s_mix[buf], 1)

                    mix(0, 0, 0)
                    mix(1, 0, K1)
                    mix(2, 0, 1)
                    with pe.Fori(1, KMAX) as a:
                        mix(1, a, a + K1)
                        mix(2, a, a + 1)
                    pe.wait_ge(s_mixe[0], 1)
                    pe.wait_ge(s_mixe[2], KMAX)
                    for i, (odd, j0, m) in enumerate(BLOCKS):
                        for j in range(2):
                            bank, turn_no = (2 * i + j) % 4, (2 * i + j) // 4 + 1
                            wait(pe, s_va[bank], turn_no - 1)
                            for b in range(8):
                                last = nc.tensor.transpose(
                                    psq[0:m * K1, bank, b * 64:(b + 1) * 64],
                                    modes[:, (odd * K1 + j0) * K1:(odd * K1 + j0 + m) * K1, 8 * j + b],
                                    ident[0:64, 0:64])
                            last.then_inc(s_v[bank], 1)

        early.close()
        with ExitStack() as two:
            def sb2(name, shape, dt=F32):
                return two.enter_context(nc.sbuf_tensor(name, shape, dt))

            def psum3(name, shape):
                return two.enter_context(nc.psum_tensor(name, shape, F32))

            NPX = NW * GC
            vin = sb2("vin", [P, K0, NC])
            usb = [sb2(f"usb{i}", [K0, NPX]) for i in range(2)]
            xn = sb2("xn", [P, 2, NPX])
            two_rows = {r: sb2(f"two_rows{r}", [P, 2, (WP if r < 16 else NW) * GC]) for r in (1,) + SCALES}
            row0 = sb2("row0", [P, 2, NC])
            edge = sb2("edge", [NC, 3, WP])
            edge3 = [sb2(f"edge3_{i}", [96, 3, NW], BF16) for i in range(2)]
            logs = {2: [sb2("log2", [P, 2 * NPX])] * 2,
                    4: [sb2("log4", [P, 2 * NPX])] * 2,
                    8: [sb2(f"log8_{i}", [P, 2 * NPX]) for i in range(2)],
                    16: [sb2("log16", [P, 2 * NPX])] * 2}
            junk = sb2("junk", [P, 2 * NPX], BF16)
            stat = sb2("stat", [P, 4 * NG])
            red = sb2("red", [32, 2])
            diag = sb2("diag", [32, 64])
            sm = sb2("sm", [P, 8, NG])
            sc1 = sb2("sc1", [P, 4])
            aff = sb2("aff", [P, 2, 2, NG])
            par = sb2("par", [P, 2, NC])
            raw = sm[:, :, :].rearrange("p a g -> p (a g)").rearrange("p (j c) -> p j c", c=NC)
            eps_k = sb2("eps_k", [P, 1])[:, :]

            psu = psum3("psu", [P, 512])
            psy = psum3("psy", [P, 2, 512])
            psm = [psum3(f"psm{i}", [P, 2, 512]) for i in range(2)]
            pst = psum3("pst", [P, 512])

            s_par = sem("params_in")
            s_pv = sem("param_steps")
            s_pa = sem("param_logs")
            s_x = [sem(f"x_in{i}") for i in range(2)]
            s_out = [sem(f"out_stored{i}") for i in range(2)]
            s_vin = sem("parts_in")
            s_u = sem("columns_done")
            s_us = sem("columns_kept")
            s_y = sem("y_done")
            s_x1 = sem("x1_done")
            s_mm = sem("min_max_done")
            s_sq = sem("x1_squared")
            s_t1 = sem("stat_sums_done")
            s_t2 = sem("extrema_spread")
            s_tv = sem("stat2_steps")
            s_ta = sem("stat2_logs")
            s_xn = sem("scaled_ready")
            s_pad = sem("pads_zeroed")
            s_p1 = sem("pairs_ready")
            s_s1 = sem("shifted_pairs_done")
            s_sc = sem("shifted_pairs_kept")
            s_w = {r: sem(f"two_row_sums{r}_ready") for r in SCALES}
            s_row = sem("row0_in")
            s_rt = sem("row0_turned")
            s_ms = {r: sem(f"measure{r}_done") for r in SCALES[1:]}
            s_l = {r: sem(f"log{r}_ready") for r in SCALES}
            s_t = sem("log4_plus_3_log2_ready")
            s_lo = sem("lower_logs_taken_off_log8")
            s_f = sem("exponent_ready")
            s_xd = sem("x1_shifted")
            s_o = sem("outputs_done")

            xs = x.rearrange("b (p q) w c -> b p (q w c)", q=2)
            os_ = out.rearrange("b (p q) w c -> b p (q w c)", q=2)

            def group(par_, g):
                return xbuf[par_].rearrange("p (m c) -> p m c", c=NC)[:, :, GC * g:GC * (g + 1)]

            def as2(ap):
                return ap.rearrange("p (m c) -> p m c", c=GC)

            def cols(ap, w0, m):
                if ap.shape[-1] == NPX:
                    return ap[:, :, w0 * GC:(w0 + m) * GC]
                return ap[:, :, (w0 + LO) * GC:(w0 + LO + m) * GC]

            def pool_sums8(k):
                return bool(ENTER[k]) or k >= STATS_AT

            def after_sample(n):
                return not (isinstance(n, int) and n == NB - 1)

            def psm_of(k, r):
                return psm[(k + SCALES.index(r) - 1) % 2]

            def add_pairs(nc_eng, eng, n, k):
                eng.wait_ge(s_xn, n * NG + (k + 1))
                wait(eng, s_w[2], n * NG + k)
                nc_eng.tensor_tensor(cols(two_rows[1], 0, NW)[:, 0, :], xn[:, 0, :], xn[:, 1, :],
                                     ALU.add).then_inc(s_p1, 1)

            def add_columns(nc_eng, eng, n, k, r):
                w0, m = SPAN[r]
                c = n * NG + k
                src = two_rows[r // 2]
                if r == 2:
                    eng.wait_ge(s_p1, c + 1)
                    eng.wait_ge(s_sc, c + 1)
                    wait(eng, s_l[2], c)
                    a, b = 0, 1
                else:
                    eng.wait_ge(s_w[r // 2], c + 1)
                    wait(eng, s_ms[r], c)
                    a, b = -STEP[r], STEP[r]
                if r < 16:
                    wait(eng, s_w[2 * r], c)
                nc_eng.tensor_tensor(cols(two_rows[r], w0, m), cols(src, w0 + a, m), cols(src, w0 + b, m),
                                     ALU.add).then_inc(s_w[r], 1)

            def walk(eng, enter, prepare, step, stats, finish=None):
                def sample(n, par_):
                    last = isinstance(n, int) and n == NB - 1
                    for k in range(NG):
                        entering = [] if last else [(n + 1, 1 - par_, g) for g in ENTER[k]]
                        after = (n, par_, k + 1) if k + 1 < NG else None if last else (n + 1, 1 - par_, 0)
                        before = (n, par_, k - 1) if k else None if isinstance(n, int) and n == 0 else \
                            (n - 1, 1 - par_, NG - 1)
                        late = (n + 1, 1 - par_, ENTER[k - 1][-1]) if not last and k and ENTER[k - 1] else None
                        step(n, par_, k, entering, before, after, late)
                        if not last and k == STATS_AT:
                            stats(n + 1, 1 - par_)

                for g in range(NG):
                    enter(0, 0, g)
                stats(0, 0)
                prepare(0, 0, 0)
                sample(0, 0)
                with eng.Fori(0, NB // 2 - 1) as two_samples:
                    sample(two_samples * 2 + 1, 1)
                    sample(two_samples * 2 + 2, 0)
                sample(NB - 1, 1)
                if finish:
                    finish(NB - 1, 1, NG - 1)

            with nc.Block() as block:
                @block.sync
                def _(sync):
                    for j, p_ in enumerate((gamma, beta, mov_mean, mov_var)):
                        sync.dma_start(raw[:, j, :], p_.rearrange("(a c) -> a c", a=1).broadcast_to([P, NC]))\
                            .then_inc(s_par, 16)

                    def load(n, par_):
                        sync.dma_start(xbuf[par_], xs[bass.ds(n, 1)].rearrange("b p m -> (b p) m"))\
                            .then_inc(s_x[par_], 16)

                    def load_parts(n):
                        wait(sync, s_u, n * NG)
                        for odd, (k0, m) in enumerate(((0, K1), (K1, KMAX))):
                            for part in range(2):
                                sync.dma_start(
                                    vin[32 * part:32 * part + K1, k0:k0 + m, :],
                                    vtab[odd].rearrange("t (a f) b c -> b t f a c", f=K1)
                                    [bass.ds(n, 1), part].rearrange("b f a c -> (b f) a c"))\
                                    .then_inc(s_vin, 16)

                    def row(n, par_):
                        sync.wait_ge(s_x1, n * NG + NG)
                        wait(sync, s_rt, n)
                        for v in range(2):
                            sync.dma_start(row0[:, v, :], xbuf[par_][0:1, v * P * NC:(v + 1) * P * NC]
                                           .rearrange("o (w c) -> o w c", c=NC)).then_inc(s_row, 16)

                    def store(n, par_):
                        sync.wait_ge(s_o, n * NG + NG)
                        sync.dma_start(os_[bass.ds(n, 1)].rearrange("b p m -> (b p) m"), xbuf[par_])\
                            .then_inc(s_out[par_], 16)

                    def turn(n, par_):
                        load_parts(n + 2)
                        row(n + 1, 1 - par_)
                        store(n, par_)
                        sync.wait_ge(s_out[par_], n * 8 + (16 - 8 * par_))
                        load(n + 2, par_)

                    sync.wait_ge(s_pad, 4)
                    load_parts(0)
                    load(1, 1)
                    load_parts(1)
                    row(0, 0)
                    turn(0, 0)
                    with sync.Fori(0, NB // 2 - 2) as two_samples:
                        turn(two_samples * 2 + 1, 1)
                        turn(two_samples * 2 + 2, 0)
                    turn(NB - 3, 1)
                    row(NB - 1, 1)
                    store(NB - 2, 0)
                    store(NB - 1, 1)
                    for par_ in range(2):
                        sync.wait_ge(s_out[par_], 16 * NB // 2)

                @block.tensor
                def _(pe):
                    pe.wait_ge(s_pad, 4)

                    def columns(n, par_, g, kept_pairs=None):
                        if g == 0:
                            pe.wait_ge(s_vin, n * 64 + 64)
                        wait(pe, s_us, n * NG + g)
                        if kept_pairs is not None:
                            pe.wait_ge(s_sc, kept_pairs)
                        for c in range(GC):
                            last = nc.tensor.matmul(psu[0:K0, c * NW:(c + 1) * NW],
                                                    vin[:, :, GC * g + c],
                                                    const(C_FI, P, NW), start=True, stop=True)
                        last.then_inc(s_u, 1)

                    def rows(n, par_, g):
                        pe.wait_ge(s_us, n * NG + (g + 1))
                        wait(pe, s_x1, n * NG + g)
                        for q in range(2):
                            last = nc.tensor.matmul(psy[:, q, :], const(C_BH + q * P, K0, P), usb[g % 2][:, :],
                                                    start=True, stop=True)
                        last.then_inc(s_y, 1)

                    def enter(n, par_, g):
                        columns(n, par_, g)
                        rows(n, par_, g)

                    def spread(n):
                        pe.wait_ge(s_tv, n * STAT_STEPS + 6)
                        nc.tensor.matmul(pst[:, 256:320], ones[0:32, :], diag[:, :],
                                         start=True, stop=True).then_inc(s_t2, 1)

                    def stats(n, par_):
                        wait(pe, s_tv, n * STAT_STEPS)
                        pe.wait_ge(s_mm, n * NG + NG)
                        pe.wait_ge(s_sq, n * NG + NG)
                        nc.tensor.matmul(pst[:, 0:32], ones, stat[:, 0:32], start=True, stop=True)
                        nc.tensor.matmul(pst[0:32, 128:256], stat[:, 32:64], ident, start=True, stop=True)\
                            .then_inc(s_t1, 1)

                    def shifted_pairs(n, k, kept=None):
                        c = n * NG + k
                        if kept is not None:
                            pe.wait_ge(s_us, kept)
                        wait(pe, s_sc, c)
                        pe.wait_ge(s_xn, c + 1)
                        for q in (1, 0):
                            last = nc.tensor.matmul(psu[:, :], band_of((2, 1, "even" if q == 0 else "odd")),
                                                    xn[:, q, :], start=(q == 1), stop=(q == 0))
                        last.then_inc(s_s1, 1)

                    def band_of(key):
                        return const(C_BAND + BAND_FOR[key] * P, P, P)

                    def measure(n, par_, k, r):
                        dst = psm_of(k, r)
                        c = n * NG + k
                        pe.wait_ge(s_w[r], c + 1)
                        before = {4: (8, 0), 8: (16, 0), 16: (4, 1)}[r]
                        wait(pe, s_l[before[0]], c + before[1])
                        nc.tensor.matmul(dst[:, 1, :], band_of((r, 1, "pair")), cols(two_rows[r], 0, NW)[:, 0, :],
                                         start=True, stop=True)
                        nc.tensor.matmul(dst[:, 0, :], band_of((r, 0, "shifted")), cols(two_rows[r], 0, NW)[:, 1, :],
                                         start=True, stop=False)
                        if k == 0 and r < 16:
                            pe.wait_ge(s_tv, n * STAT_STEPS + (EDGE4_READY if r == 4 else STAT_STEPS))
                        i = SCALES.index(r) - 1
                        for ch in range(GC):
                            at = 4 * (GC * k + ch)
                            nc.tensor.matmul(dst[0:4, 0, ch:NPX:GC], sel[:, i, at:at + 4],
                                             edge3[par_][:, i, :], start=False, stop=False)
                        nc.tensor.matmul(dst[:, 0, :], sel[0:1, 3, :], sel[0:1, :, :].rearrange("p a m -> p (a m)"),
                                         start=False, stop=True).then_inc(s_ms[r], 1)

                    def turn_row0(n):
                        pe.wait_ge(s_tv, n * STAT_STEPS + ROW_SCALED)
                        for v in range(2):
                            last = nc.tensor.transpose(pst[0:NC, 128 + P * v:128 + P * (v + 1)],
                                                       row0[:, v, :], ident)
                        last.then_inc(s_rt, 1)

                    def prepare(n, par_, k):
                        spread(n)
                        turn_row0(n)
                        shifted_pairs(n, k, n * NG + NG)

                    def step(n, par_, k, entering, before, after, late):
                        c = n * NG + k
                        kept = entering[0][0] * NG + entering[0][2] + 1 if entering else None
                        if entering:
                            columns(*entering[0], c + 1)
                        measure(n, par_, k, 4)
                        if entering:
                            rows(*entering[0])
                        if k == STATS_AT + 1 and after_sample(n):
                            spread(n + 1)
                        if after:
                            shifted_pairs(after[0], after[2], kept)
                        if len(entering) > 2:
                            columns(*entering[1], c + 2)
                        measure(n, par_, k, 8)
                        if k == STATS_AT + 2 and after_sample(n):
                            turn_row0(n + 1)
                        if len(entering) > 2:
                            rows(*entering[1])
                        if entering:
                            columns(*entering[-1], c + 2)
                        measure(n, par_, k, 16)
                        if entering:
                            rows(*entering[-1])

                    walk(pe, enter, prepare, step, stats)

                @block.scalar
                def _(act):
                    act.wait_ge(s_pv, 1)
                    nc.scalar.activation(par[:, 0, :], raw[:, 3, :], ACT.Ln).then_inc(s_pa, 1)
                    act.wait_ge(s_pa, 1)
                    nc.scalar.activation(par[:, 0, :], par[:, 0, :], ACT.Exp, scale=-0.5).then_inc(s_pa, 1)
                    act.wait_ge(s_pad, 4)

                    def keep(n, par_, g):
                        act.wait_ge(s_u, n * NG + (g + 1))
                        wait(act, s_y, n * NG + (g - 1))
                        nc.scalar.activation(usb[g % 2][:, :].rearrange("p (w c) -> p c w", c=GC),
                                             psu[0:K0, :].rearrange("p (c w) -> p c w", c=GC),
                                             ACT.Copy).then_inc(s_us, 1)

                    def square(n, par_, g):
                        act.wait_ge(s_x1, n * NG + (g + 1))
                        if g == 0:
                            wait(act, s_t1, n)
                        wait(act, s_sq, n * NG + g)
                        nc.scalar.activation(as2(junk[:, :]), group(par_, g), ACT.Square,
                                             accum_out=stat[:, NG + g:NG + g + 1]).then_inc(s_sq, 1)

                    def enter(n, par_, g):
                        keep(n, par_, g)
                        square(n, par_, g)

                    def roots(n):
                        act.wait_ge(s_tv, n * STAT_STEPS + 9)
                        nc.scalar.activation(sm[:, 4, :], sm[:, 3, :], ACT.Ln).then_inc(s_ta, 1)
                        act.wait_ge(s_ta, n * 2 + 1)
                        nc.scalar.activation(sm[:, 4, :], sm[:, 4, :], ACT.Exp, scale=-0.5).then_inc(s_ta, 1)

                    def keep_pairs(n, k):
                        act.wait_ge(s_s1, n * NG + (k + 1))
                        wait(act, s_w[2], n * NG + k)
                        nc.scalar.activation(cols(two_rows[1], 0, NW)[:, 1, :], psu[:, :], ACT.Copy)\
                            .then_inc(s_sc, 1)

                    def prepare(n, par_, k):
                        roots(n)
                        scaled(n, par_, k)
                        keep_pairs(n, k)

                    def scaled(n, par_, k):
                        if k == 0:
                            act.wait_ge(s_tv, n * STAT_STEPS + SCALE_READY)
                        wait(act, s_p1, n * NG + k)
                        wait(act, s_s1, n * NG + k)
                        nc.scalar.activation(
                            xn[:, :, :].rearrange("p q (w c) -> p q w c", c=GC),
                            group(par_, k).rearrange("p (q w) c -> p q w c", q=2),
                            ACT.Relu, scale=aff[:, par_, 0, k:k + 1], bias=aff[:, par_, 1, k:k + 1])\
                            .then_inc(s_xn, 1)

                    def log(n, par_, k, r):
                        dst = logs[r][k % 2]
                        c = n * NG + k
                        if r == 2:
                            wait(act, s_lo, c)
                        elif r == 4:
                            wait(act, s_t, c)
                        elif r == 8:
                            wait(act, s_o, c - 1)
                        else:
                            wait(act, s_f, c)
                        if r == 2:
                            act.wait_ge(s_w[2], c + 1)
                            nc.scalar.activation(dst[:, :].rearrange("p (e m) -> p e m", e=2),
                                                 cols(two_rows[2], 0, NW), ACT.Ln, bias=eps_k).then_inc(s_l[2], 1)
                        else:
                            act.wait_ge(s_ms[r], c + 1)
                            nc.scalar.activation(
                                dst[:, :], psm_of(k, r)[:, :, :].rearrange("p e m -> p (e m)"),
                                ACT.Ln, bias=eps_k).then_inc(s_l[r], 1)

                    def step(n, par_, k, entering, before, after, late):
                        if entering:
                            keep(*entering[0])
                        if before:
                            log(*before, 16)
                        if after:
                            scaled(*after)
                        log(n, par_, k, 2)
                        if k == STATS_AT + 1 and after_sample(n):
                            roots(n + 1)
                        if late:
                            square(*late)
                        log(n, par_, k, 4)
                        if after:
                            keep_pairs(after[0], after[2])
                        if len(entering) > 2:
                            keep(*entering[1])
                        log(n, par_, k, 8)
                        if entering:
                            square(*entering[0])
                            keep(*entering[-1])
                        if len(entering) > 2:
                            square(*entering[1])

                    walk(act, enter, prepare, step, lambda *a: None, lambda *a: log(*a, 16))

                @block.vector
                def _(dve):
                    steps = [0]

                    def plink(ins):
                        steps[0] += 1
                        ins.then_inc(s_pv, 1)
                        dve.wait_ge(s_pv, steps[0])

                    nc.vector.memset(eps_k, EPS_K).then_inc(s_pad, 1)
                    nc.vector.memset(two_rows[1][:, :, :], 0.0).then_inc(s_pad, 1)
                    nc.vector.memset(vin[:, :, :], 0.0).then_inc(s_pad, 1)
                    nc.vector.memset(edge[:, :, :], 0.0).then_inc(s_pad, 1)
                    dve.wait_ge(s_pad, 4)
                    dve.wait_ge(s_par, 64)
                    ga, be, mm_, va = (raw[:, j, :] for j in range(4))
                    kc, dc = par[:, 0, :], par[:, 1, :]
                    plink(nc.vector.tensor_scalar(va, va, EPS_BN, None, ALU.add))
                    dve.wait_ge(s_pa, 2)
                    plink(nc.vector.tensor_tensor(dc, kc, kc, ALU.mult))
                    plink(nc.vector.tensor_tensor(dc, dc, va, ALU.mult))
                    plink(nc.vector.tensor_scalar(dc, dc, -0.5, 1.5, ALU.mult, ALU.add))
                    plink(nc.vector.tensor_tensor(kc, kc, dc, ALU.mult))
                    plink(nc.vector.tensor_tensor(kc, kc, ga, ALU.mult))
                    plink(nc.vector.tensor_tensor(dc, kc, mm_, ALU.mult))
                    plink(nc.vector.tensor_tensor(dc, be, dc, ALU.subtract))
                    plink(nc.vector.tensor_scalar(kc, kc, 1.0 / (10.0 * LN2), None, ALU.mult))
                    assert steps[0] == PARAM_STEPS

                    def add(n, par_, g):
                        if g == 0:
                            wait(dve, s_x[par_], n * 8 - 8 * par_ + 16 * par_)
                            wait(dve, s_t1, n)
                        dve.wait_ge(s_y, n * NG + (g + 1))
                        nc.vector.scalar_tensor_tensor(
                            group(par_, g), group(par_, g), 1.0,
                            as2(psy[:, :, :].rearrange("p q m -> p (q m)")), ALU.mult, ALU.add,
                            accum_out=stat[:, g:g + 1]).then_inc(s_x1, 1)

                    def extrema(n, par_, g):
                        dve.wait_ge(s_x1, n * NG + (g + 1))
                        for j, op in ((2, ALU.min), (3, ALU.max)):
                            last = nc.vector.tensor_reduce(stat[:, j * NG + g:j * NG + g + 1],
                                                           group(par_, g), mybir.AxisListType.XY, op)
                        last.then_inc(s_mm, 1)

                    def enter(n, par_, g):
                        add(n, par_, g)
                        extrema(n, par_, g)

                    def linker(n, done):
                        def link(ins):
                            done[0] += 1
                            ins.then_inc(s_tv, 1)
                            dve.wait_ge(s_tv, n * STAT_STEPS + done[0])
                        return link

                    mean, ex2, t, ve, r0, s, lo, hi = (sm[:, j, :] for j in range(8))

                    def stats(n, par_):
                        k = [0]
                        link = linker(n, k)
                        dve.wait_ge(s_t1, n + 1)
                        ext = pst[0:32, 128:256]
                        link(nc.vector.tensor_reduce(red[:, 0:1], ext, X_AXIS, ALU.min))
                        link(nc.vector.tensor_reduce(red[:, 1:2], ext, X_AXIS, ALU.max))
                        for j in range(2):
                            link(nc.vector.tensor_scalar(diag[:, 32 * j:32 * j + 32], ident[0:32, 0:32],
                                                         red[:, j:j + 1], None, ALU.mult))
                        link(nc.vector.tensor_scalar(mean, pst[:, 0:16], 1.0 / GROUP, None, ALU.mult))
                        link(nc.vector.tensor_scalar(ex2, pst[:, 16:32], 1.0 / GROUP, None, ALU.mult))
                        link(nc.vector.tensor_tensor(t, mean, mean, ALU.mult))
                        link(nc.vector.tensor_tensor(ve, ex2, t, ALU.subtract))
                        link(nc.vector.tensor_scalar(ve, ve, 0.0, EPS_GN, ALU.max, ALU.add))
                        assert k[0] == 9, k[0]

                    def stats_end(n, par_):
                        k = [9]
                        link = linker(n, k)
                        dve.wait_ge(s_ta, n * 2 + 2)
                        link(nc.vector.tensor_tensor(t, r0, r0, ALU.mult))
                        link(nc.vector.tensor_tensor(t, t, ve, ALU.mult))
                        link(nc.vector.tensor_scalar(t, t, -0.5, 1.5, ALU.mult, ALU.add))
                        link(nc.vector.tensor_tensor(s, r0, t, ALU.mult))
                        dve.wait_ge(s_t2, n + 1)
                        link(nc.vector.tensor_tensor(lo, pst[:, 256:272], mean, ALU.subtract))
                        link(nc.vector.tensor_tensor(lo, lo, s, ALU.mult))
                        link(nc.vector.tensor_tensor(hi, pst[:, 304:320], mean, ALU.subtract))
                        link(nc.vector.tensor_tensor(hi, hi, s, ALU.mult))
                        mn, mx, inv = sc1[:, 0:1], sc1[:, 1:2], sc1[:, 2:3]
                        link(nc.vector.tensor_reduce(mn, lo, X_AXIS, ALU.min))
                        link(nc.vector.tensor_reduce(mx, hi, X_AXIS, ALU.max))
                        link(nc.vector.tensor_tensor(mx, mx, mn, ALU.subtract))
                        link(nc.vector.tensor_scalar(mx, mx, EPS_K, None, ALU.add))
                        link(nc.vector.reciprocal(inv, mx))
                        link(nc.vector.tensor_tensor(t, mean, s, ALU.mult))
                        link(nc.vector.tensor_scalar(t, t, mn, -1.0, ALU.add, ALU.mult))
                        link(nc.vector.tensor_scalar(aff[:, par_, 0, :], s, inv, None, ALU.mult))
                        link(nc.vector.tensor_scalar(aff[:, par_, 1, :], t, inv, None, ALU.mult))
                        dve.wait_ge(s_row, n * 32 + 32)
                        row0_g = row0[:, :, :].rearrange("p v (g c) -> p v g c", c=GC)
                        scale, bias = (aff[:, par_, j:j + 1, :].rearrange("p v (g c) -> p v g c", c=1)
                                       .broadcast_to([P, 2, NG, GC]) for j in range(2))
                        link(nc.vector.tensor_tensor(row0_g, row0_g, scale, ALU.mult))
                        link(nc.vector.tensor_tensor(row0_g, row0_g, bias, ALU.add))
                        link(nc.vector.tensor_scalar(row0[:, :, :], row0[:, :, :], 0.0, None, ALU.max))
                        assert k[0] == ROW_SCALED, k[0]

                    def edge_sums(n, par_):
                        k = [ROW_SCALED]
                        link = linker(n, k)
                        dve.wait_ge(s_rt, n + 1)

                        def span(j, w0, m):
                            return edge[:, j, LO + w0:LO + w0 + m]

                        link(nc.vector.tensor_copy(span(2, 0, NW), pst[0:NC, 128:384]))
                        for dst, src, r in ((1, 2, 2), (0, 1, 4), (1, 0, 8), (2, 1, 16)):
                            w0, m = SPAN[r]
                            a, b = (0, 1) if r == 2 else (-STEP[r], STEP[r])
                            link(nc.vector.tensor_tensor(span(dst, w0, m), span(src, w0 + a, m),
                                                         span(src, w0 + b, m), ALU.add))
                        wait(dve, s_ms[16], n * NG - NG if not isinstance(n, int) or n > 1 else 0)
                        edge_parts(n, par_, 0, 1, k)
                        assert k[0] == EDGE4_READY, k[0]

                    def edge_parts(n, par_, j0, j1, k):
                        link = linker(n, k)
                        sums_ = edge[:, j0:j1, LO:LO + NW]
                        for part in range(2):
                            dst = edge3[par_][32 * part:32 * part + 32, j0:j1]
                            link(nc.vector.tensor_copy(dst, sums_))
                            rest = sums_ if part == 0 else edge3[par_][64:96, j0:j1]
                            link(nc.vector.tensor_tensor(rest, sums_, dst, ALU.subtract))

                    def edge_rest(n, par_):
                        k = [EDGE4_READY]
                        edge_parts(n, par_, 1, 3, k)
                        assert k[0] == STAT_STEPS, k[0]

                    def sums(n, k, r):
                        add_columns(nc.vector, dve, n, k, r)

                    def prepare(n, par_, k):
                        stats_end(n, par_)
                        add_pairs(nc.vector, dve, n, k)
                        edge_sums(n, par_)
                        sums(n, k, 2)
                        sums(n, k, 4)
                        sums(n, k, 8)
                        edge_rest(n, par_)

                    def lower(n, k):
                        l2, l4 = logs[2][0][:, :], logs[4][0][:, :]
                        dve.wait_ge(s_l[2], n * NG + (k + 1))
                        dve.wait_ge(s_l[4], n * NG + (k + 1))
                        nc.vector.scalar_tensor_tensor(l2, l2, 3.0, l4, ALU.mult, ALU.add).then_inc(s_t, 1)

                    def exponent(n, par_, k):
                        l8, l16 = logs[8][k % 2][:, :], logs[16][0][:, :]
                        dve.wait_ge(s_lo, n * NG + (k + 1))
                        dve.wait_ge(s_l[16], n * NG + (k + 1))
                        nc.vector.scalar_tensor_tensor(l8, l16, 3.0, l8, ALU.mult, ALU.add).then_inc(s_f, 1)

                    def output(n, par_, k):
                        dve.wait_ge(s_f, n * NG + (k + 1))
                        dve.wait_ge(s_xd, n * NG + (k + 1))
                        for c in range(GC):
                            dst = group(par_, k)[:, :, c]
                            last = nc.vector.scalar_tensor_tensor(
                                dst, as2(logs[8][k % 2][:, :])[:, :, c], kc[:, GC * k + c:GC * k + c + 1],
                                dst, ALU.mult, ALU.add)
                        last.then_inc(s_o, 1)

                    def step(n, par_, k, entering, before, after, late):
                        if late:
                            add(*late)
                            extrema(*late)
                        if after and not entering:
                            add_pairs(nc.vector, dve, after[0], after[2])
                        if before:
                            exponent(*before)
                            output(*before)
                        lower(n, k)
                        if entering:
                            add(*entering[0])
                        if after:
                            sums(after[0], after[2], 2)
                        if after and not entering:
                            sums(after[0], after[2], 4)
                        if after and not pool_sums8(k):
                            sums(after[0], after[2], 8)
                        if entering:
                            extrema(*entering[0])
                        if len(entering) > 2:
                            add(*entering[1])
                            extrema(*entering[1])
                        if k == STATS_AT + 1 and after_sample(n):
                            stats_end(n + 1, 1 - par_)
                        if k == STATS_AT + 2 and after_sample(n):
                            edge_sums(n + 1, 1 - par_)
                        if k == STATS_AT + 3 and after_sample(n):
                            edge_rest(n + 1, 1 - par_)

                    def finish(n, par_, k):
                        exponent(n, par_, k)
                        output(n, par_, k)

                    walk(dve, enter, prepare, step, stats, finish)

                @block.gpsimd
                def _(pool):
                    pool.wait_ge(s_pv, PARAM_STEPS)

                    def shift(n, par_, k):
                        pool.wait_ge(s_xn, n * NG + (k + 1))
                        if k == 0:
                            pool.wait_ge(s_row, n * 32 + 32)
                        dc = par[:, 1:2, GC * k:GC * (k + 1)].broadcast_to([P, 2 * NW, GC])
                        nc.gpsimd.tensor_tensor(group(par_, k), group(par_, k), dc, ALU.add)\
                            .then_inc(s_xd, 1)

                    def take_lower(n, k):
                        pool.wait_ge(s_t, n * NG + (k + 1))
                        pool.wait_ge(s_l[8], n * NG + (k + 1))
                        l8 = logs[8][k % 2][:, :]
                        nc.gpsimd.tensor_tensor(l8, l8, logs[2][0][:, :], ALU.subtract).then_inc(s_lo, 1)

                    def step(n, par_, k, entering, before, after, late):
                        if after and entering:
                            add_pairs(nc.gpsimd, pool, after[0], after[2])
                        add_columns(nc.gpsimd, pool, n, k, 16)
                        shift(n, par_, k)
                        if after and entering:
                            add_columns(nc.gpsimd, pool, after[0], after[2], 4)
                        take_lower(n, k)
                        if after and pool_sums8(k):
                            add_columns(nc.gpsimd, pool, after[0], after[2], 8)

                    walk(pool, lambda *a: None, lambda *a: None, step, lambda *a: None)


SLOT_STEPS = 14
MID_STEPS = 10
PARAM_STEPS = 9
SCALE_READY = 26
ROW_SCALED = SCALE_READY + 3
EDGE4_READY = ROW_SCALED + 9
STAT_STEPS = EDGE4_READY + 4

_INS = ["x", "L0_conv_w_re", "L0_conv_w_im", "L0_conv_idx0", "L0_conv_idx1", "L1_conv_gamma",
        "L1_conv_beta", "L1_conv_moving_mean", "L1_conv_moving_var"]


def kernel(**inputs):
    import concourse.bacc as _bacc
    from concourse.bass_utils import run_bass_kernel_spmd as _run

    nc = _bacc.Bacc("TRN2", target_bir_lowering=False, num_devices=1)
    arrays, args = {}, []
    for name in _INS:
        a = np.ascontiguousarray(inputs[name])
        arrays[f"in_{name}"] = a
        args.append(nc.dram_tensor(f"in_{name}", a.shape, mybir.dt.from_np(a.dtype), kind="ExternalInput").ap())
    table = constants()
    arrays["in_table"] = table
    args.append(nc.dram_tensor("in_table", table.shape, F32, kind="ExternalInput").ap())
    args.append(nc.dram_tensor("out_0", (NB, NH, NW, NC), F32, kind="ExternalOutput").ap())
    build(nc, *args)
    r = _run(nc, [arrays], core_ids=[0])
    return r.results[0]["out_0"]
```
